# Optimizing a Trainium2 kernel written in Bass

```python
import numpy as np
import jax
import jax.numpy as jnp

def _softmax(x, axis=-1):
    return jax.nn.softmax(x, axis=axis)

def _gelu(x):
    return jax.nn.gelu(x, approximate=True)

def _silu(x):
    return jax.nn.silu(x)

def _sigmoid(x):
    return jax.nn.sigmoid(x)

def _layernorm(x, axis=-1, eps=1e-05):
    m = jnp.mean(x, axis=axis, keepdims=True)
    v = jnp.var(x, axis=axis, keepdims=True)
    return (x - m) / jnp.sqrt(v + eps)

def _scatter_add(tgt, idx, src, axis=0):
    return tgt.at[idx].add(src)

def _segment_sum(src, seg, n):
    return jax.ops.segment_sum(src, seg, n)
kernel_name = 'mk_sandwich_d1_jaxref_r8_dd99a0'

def setup_inputs(seed: int=0):
    np.random.seed(seed)
    _w = jnp.asarray

    def _L0_attn_setup():
        import jax, jax.numpy as jnp
        import numpy as np
        B, T, HID = (2, 256, 128)
        H, HKV, D = (16, 4, 64)
        GLR = 16
        GATE_LOGIT_NORMALIZER = 16.0
        EPS = 1e-06

        def _gla(q, k, v, g):
            scale = q.shape[-1] ** (-0.5)
            qs = jnp.moveaxis(q * scale, 2, 0)
            ks_ = jnp.moveaxis(k, 2, 0)
            vs = jnp.moveaxis(v, 2, 0)
            gs = jnp.moveaxis(g, 2, 0)
            S0 = jnp.zeros(q.shape[:2] + (q.shape[-1], v.shape[-1]), q.dtype)

            def step(S, inp):
                qt, kt, vt, gt = inp
                S = jnp.exp(gt)[..., None] * S + kt[..., None] * vt[..., None, :]
                o = jnp.einsum('bhk,bhkv->bhv', qt, S)
                return (S, o)
            S, o = jax.lax.scan(step, S0, (qs, ks_, vs, gs))
            return (jnp.moveaxis(o, 0, 2), S)
        key = jax.random.key(seed)
        ks = jax.random.split(key, 8)
        w = lambda k, shape: jax.random.normal(k, shape, jnp.float32) * 0.02
        return dict(hidden_states=jax.random.normal(ks[0], (B, T, HID), jnp.float32), Wq=w(ks[1], (HID, H * D)), Wk=w(ks[2], (HID, HKV * D)), Wv=w(ks[3], (HID, HKV * D)), Wo=w(ks[4], (H * D, HID)), Wg1=w(ks[5], (HID, GLR)), Wg2=w(ks[6], (GLR, HKV * D)), bg2=jnp.zeros((HKV * D,), jnp.float32), g_norm_weight=jnp.ones((D,), jnp.float32))
    _L0_attn_in = _L0_attn_setup()

    def _L0_ffn_setup():
        import jax, jax.numpy as jnp
        import numpy as np
        TOP_K = 2
        NUM_EXPERTS = 8
        B, T, H, F = (4, 256, 128, 512)
        key = jax.random.key(seed)
        ks = jax.random.split(key, 6)
        s_in = 1.0 / np.sqrt(H)
        s_ff = 1.0 / np.sqrt(F)
        return {'x': jax.random.normal(ks[0], (B, T, H), dtype=jnp.float32), 'router_w': jax.random.normal(ks[1], (NUM_EXPERTS, H), dtype=jnp.float32) * s_in, 'router_b': jax.random.normal(ks[2], (NUM_EXPERTS,), dtype=jnp.float32) * 0.01, 'gate_w': jax.random.normal(ks[3], (NUM_EXPERTS, F, H), dtype=jnp.float32) * s_in, 'up_w': jax.random.normal(ks[4], (NUM_EXPERTS, F, H), dtype=jnp.float32) * s_in, 'down_w': jax.random.normal(ks[5], (NUM_EXPERTS, H, F), dtype=jnp.float32) * s_ff}
    _L0_ffn_in = _L0_ffn_setup()
    _d = {'L0_attn_hidden_states': _L0_attn_in['hidden_states'], 'L0_attn_Wq': _L0_attn_in['Wq'], 'L0_attn_Wk': _L0_attn_in['Wk'], 'L0_attn_Wv': _L0_attn_in['Wv'], 'L0_attn_Wo': _L0_attn_in['Wo'], 'L0_attn_Wg1': _L0_attn_in['Wg1'], 'L0_attn_Wg2': _L0_attn_in['Wg2'], 'L0_attn_bg2': _L0_attn_in['bg2'], 'L0_attn_g_norm_weight': _L0_attn_in['g_norm_weight'], 'L0_ffn_router_w': _L0_ffn_in['router_w'], 'L0_ffn_router_b': _L0_ffn_in['router_b'], 'L0_ffn_gate_w': _L0_ffn_in['gate_w'], 'L0_ffn_up_w': _L0_ffn_in['up_w'], 'L0_ffn_down_w': _L0_ffn_in['down_w']}
    _x0 = _d['L0_attn_hidden_states']
    _d['L0_attn_hidden_states'] = jax.random.normal(jax.random.fold_in(jax.random.key(seed), 1), (16, 512, 128), dtype=_x0.dtype)
    del _x0
    return _d

def reference(L0_attn_hidden_states, L0_attn_Wq, L0_attn_Wk, L0_attn_Wv, L0_attn_Wo, L0_attn_Wg1, L0_attn_Wg2, L0_attn_bg2, L0_attn_g_norm_weight, L0_ffn_router_w, L0_ffn_router_b, L0_ffn_gate_w, L0_ffn_up_w, L0_ffn_down_w):

    def _L0_attn_ref(hidden_states, Wq, Wk, Wv, Wo, Wg1, Wg2, bg2, g_norm_weight):
        import jax, jax.numpy as jnp
        import numpy as np
        B, T, HID = (2, 256, 128)
        H, HKV, D = (16, 4, 64)
        GLR = 16
        GATE_LOGIT_NORMALIZER = 16.0
        EPS = 1e-06

        def _gla(q, k, v, g):
            scale = q.shape[-1] ** (-0.5)
            qs = jnp.moveaxis(q * scale, 2, 0)
            ks_ = jnp.moveaxis(k, 2, 0)
            vs = jnp.moveaxis(v, 2, 0)
            gs = jnp.moveaxis(g, 2, 0)
            S0 = jnp.zeros(q.shape[:2] + (q.shape[-1], v.shape[-1]), q.dtype)

            def step(S, inp):
                qt, kt, vt, gt = inp
                S = jnp.exp(gt)[..., None] * S + kt[..., None] * vt[..., None, :]
                o = jnp.einsum('bhk,bhkv->bhv', qt, S)
                return (S, o)
            S, o = jax.lax.scan(step, S0, (qs, ks_, vs, gs))
            return (jnp.moveaxis(o, 0, 2), S)
        b, t, _ = hidden_states.shape
        split = lambda x, h: jnp.transpose(x.reshape(b, t, h, D), (0, 2, 1, 3))
        q = jax.nn.relu(split(hidden_states @ Wq, H))
        k = jax.nn.relu(split(hidden_states @ Wk, HKV))
        v = split(hidden_states @ Wv, HKV)
        gk = jax.nn.log_sigmoid(split(hidden_states @ Wg1 @ Wg2 + bg2, HKV)) / GATE_LOGIT_NORMALIZER
        rep = lambda x: jnp.repeat(x, H // HKV, axis=1)
        o, _ = _gla(q, rep(k), rep(v), rep(gk))
        o = jnp.transpose(o, (0, 2, 1, 3))
        var = jnp.mean(jnp.square(o), axis=-1, keepdims=True)
        o = g_norm_weight * (o * jax.lax.rsqrt(var + EPS))
        return o.reshape(b, t, H * D) @ Wo

    def _L0_ffn_ref(x, router_w, router_b, gate_w, up_w, down_w):
        import jax, jax.numpy as jnp
        import numpy as np
        TOP_K = 2
        NUM_EXPERTS = 8
        B, T, H, F = (4, 256, 128, 512)
        logits = jnp.einsum('bth,eh->bte', x, router_w) + router_b
        topv, topi = jax.lax.top_k(logits, TOP_K)
        gates = jax.nn.softmax(topv, axis=-1)

        def body(acc, inputs):
            e, gw, uw, dw = inputs
            w = jnp.sum(gates * (topi == e), axis=-1)
            h = jax.nn.silu(jnp.einsum('bth,fh->btf', x, gw)) * jnp.einsum('bth,fh->btf', x, uw)
            y = jnp.einsum('btf,hf->bth', h, dw)
            return (acc + y * w[..., None], None)
        init = jnp.zeros_like(x)
        xs = (jnp.arange(NUM_EXPERTS), gate_w, up_w, down_w)
        out, _ = jax.lax.scan(body, init, xs)
        return out
    x = L0_attn_hidden_states
    x = x + _layernorm(_L0_attn_ref(_layernorm(x, axis=-1), L0_attn_Wq, L0_attn_Wk, L0_attn_Wv, L0_attn_Wo, L0_attn_Wg1, L0_attn_Wg2, L0_attn_bg2, L0_attn_g_norm_weight), axis=-1)
    x = x + _layernorm(_L0_ffn_ref(_layernorm(x, axis=-1), L0_ffn_router_w, L0_ffn_router_b, L0_ffn_gate_w, L0_ffn_up_w, L0_ffn_down_w), axis=-1)
    return x

_drawn_inputs = setup_inputs


def setup_inputs(seed=0):
    import zlib

    import numpy as np

    out = dict(_drawn_inputs(seed))
    spreads = {'L0_attn_bg2': (0.0, 0.1), 'L0_attn_g_norm_weight': (1.0, 0.2)}
    factors = {'L0_attn_Wg1': 6.342, 'L0_attn_Wg2': 5.695}
    for name, (base, spread) in spreads.items():
        noise = np.random.default_rng([zlib.crc32(name.encode()), seed]).standard_normal(out[name].shape)
        drawn = base * np.exp(spread * noise) if base else spread * noise
        out[name] = jnp.asarray(drawn.astype(out[name].dtype))
    for name, factor in factors.items():
        out[name] = (out[name] * factor).astype(out[name].dtype)
    return out
```

```python
from contextlib import ExitStack

import numpy as np

import concourse.bass as bass
from concourse import mybir

P = 128
F32 = mybir.dt.float32
U32 = mybir.dt.uint32
I32 = mybir.dt.int32
BF16 = mybir.dt.bfloat16
ALU = mybir.AluOpType
ACT = mybir.ActivationFunctionType
LOG_EXP = "natural_log_exp_and_others"
AX = mybir.AxisListType.X

D = 64
C = 64
HID = 128
LOW = 16
PAIRS = 2
R = 4
E = 8
FF = 512
FB = FF // P
ROWS = 256
NORM_EPS = 1e-6
LN_EPS = 1e-5
GATE_NORMALIZER = 16.0

C_IDENT, C_MASK, C_TRI, C_IOTA, C_SCAN = 0, 128, 192, 320, 328
C_EPS_HEAD, C_EPS_LN = C_SCAN + 1024, C_SCAN + 1025
C_BASE = C_SCAN + 1026
C_ONES = C_BASE + 8
C_TNUM = C_ONES + 8



def build(nc, x, wq, wk, wv, wo, wg1, wg2, bg2, gnorm, rw, rb, wgate, wup, wdown, consts, out):
    S, L, _ = x.shape
    NC = L // C
    NT = L // P
    T = S * L
    CAP = T + ROWS
    TILES = 2 * T // ROWS + E

    ctx = ExitStack()
    with ctx:
        def sb(name, shape, dt=F32):
            return ctx.enter_context(nc.sbuf_tensor(name, shape, dt))

        def ps(name, shape):
            return ctx.enter_context(nc.psum_tensor(name, shape, F32))

        def sem(name):
            return ctx.enter_context(nc.semaphore(name))

        xs_dram = nc.dram_tensor("expert_rows", (E * CAP + ROWS, HID), F32).ap()
        ys_dram = nc.dram_tensor("expert_out", (TILES * ROWS, HID), F32).ap()
        x1_dram = nc.dram_tensor("after_attention", (T, HID), F32).ap()

        cst = sb("cst", [P, C_TNUM + TILES + 1])
        wq_sb = sb("wq_sb", [P, PAIRS, R, P])
        wk_sb = sb("wk_sb", [P, PAIRS, P])
        wv_sb = sb("wv_sb", [P, 2 * PAIRS * D])
        wo_sb = sb("wo_sb", [P, PAIRS * R, HID])
        wg1_sb = sb("wg1_sb", [P, LOW])
        wg2_sb = sb("wg2_sb", [LOW, PAIRS, P])
        bg2_sb = sb("bg2_sb", [P, PAIRS])
        gn_sb = sb("gn_sb", [P, 1])
        rw_sb = sb("rw_sb", [P, E])
        rb_sb = sb("rb_sb", [P, E])
        wgate_sb = sb("wgate_sb", [P, E, FF])
        wup_sb = sb("wup_sb", [P, E, FF])
        wdown_sb = sb("wdown_sb", [P, E, FB, HID])
        ident = cst[:, C_IDENT:C_IDENT + P]
        causal = cst[:, C_MASK:C_MASK + C]
        iota8 = cst[:, C_IOTA:C_IOTA + E]
        tnum = cst[0:1, C_TNUM:C_TNUM + TILES + 1]
        ones_row = cst[:, C_ONES:C_ONES + E]
        in_chunk = cst[:, C_SCAN:C_SCAN + 1024]
        tri = sb("tri", [P, P], BF16)
        ones = sb("ones", [P, P], BF16)
        zeros = sb("zeros", [P, ROWS // P * HID])

        xa = sb("xa", [P, NT, HID])
        xr = sb("xr", [P, NT, HID])
        xn = sb("xn", [P, NT, HID])
        xnT = sb("xnT", [P, NC, 2, C])
        h1 = sb("h1", [LOW, L])
        absz = sb("absz", [P, PAIRS, L])
        minz = sb("minz", [P, PAIRS, L])
        run = sb("run", [P, PAIRS, L])
        rel = sb("rel", [P, PAIRS, L])
        grow = sb("grow", [P, PAIRS, L])
        shrink = sb("shrink", [P, PAIRS, L])
        step_log = sb("step_log", [P, PAIRS, NC])
        step = sb("step", [P, PAIRS, NC])
        qT = sb("qT", [P, PAIRS, NC, R, C])
        kT = sb("kT", [P, PAIRS, NC, P])
        kJ = sb("kJ", [P, NC, PAIRS, P])
        vJ = sb("vJ", [P, NC, PAIRS, P])
        S_raw = sb("S_raw", [P, 2, PAIRS, P])
        S_mid = sb("S_mid", [P, NC, PAIRS, P])
        aT = sb("aT", [P, 2, PAIRS, R * C])
        sq = sb("sq", [P, 2, 512])
        ss = sb("ss", [P, 2, 8])
        lnss = sb("lnss", [P, 2, 8])
        rs = sb("rs", [P, 2, 8])
        on = sb("on", [P, 2, 4, P])
        oT = sb("oT", [P, 2, PAIRS * R, 2, C])
        st = sb("st", [P, 3, NT, 6])
        mv = sb("mv", [P, 3, NT, 2])
        lnv = sb("lnv", [P, 3, NT])
        rstd = sb("rstd", [P, 3, NT])
        an = sb("an", [P, NT, HID])
        x1 = sb("x1", [P, NT, HID])
        x1n = sb("x1n", [P, NT, HID])
        x1nT = sb("x1nT", [P, NT, P])

        logit = sb("logit", [P, NT, E])
        top = sb("top", [P, NT, 8])
        top_i = sb("top_i", [P, NT, 8], U32)
        top_f = sb("top_f", [P, NT, 8])
        pick = sb("pick", [P, 2, NT, E])
        both = sb("both", [P, NT, E], BF16)
        place = sb("place", [P, NT, E])
        base = sb("base", [P, E])
        placed = sb("placed", [P, 2, NT, E])
        rowf = sb("rowf", [P, 2, NT])
        rowi = sb("rowi", [P, 2, NT], U32)
        diff = sb("diff", [P, NT])
        ediff = sb("ediff", [P, NT])
        den = sb("den", [P, NT])
        gts = sb("gts", [P, 2, NT])
        rows_all = sb("rows_all", [P, S, 2 * NT])
        expert_all = sb("expert_all", [P, S, 2 * NT])
        gates_all = sb("gates_all", [P, S, 2 * NT])

        cnt = sb("cnt", [P, E])
        cnt_i = sb("cnt_i", [P, E], I32)
        til_i = sb("til_i", [P, E], I32)
        til = sb("til", [P, E])
        cum = sb("cum", [P, E])
        cum_i = sb("cum_i", [P, E], U32)
        end_i = sb("end_i", [P, E], U32)
        shift = sb("shift", [P, E])
        tge = sb("tge", [1, TILES + 1, E])
        tmul = sb("tmul", [1, TILES + 1, E])
        te = sb("te", [1, TILES + 1])
        tprev = sb("tprev", [1, TILES + 1])
        trow = sb("trow", [1, TILES + 1])
        trow_i = sb("trow_i", [1, TILES + 1], U32)
        chosen = qT[:].rearrange("p a n r c -> p (a n r c)")[:, 0:S * 2 * NT * E].rearrange("p (n e) -> p n e", e=E)
        result_f = sb("result_f", [P, S * 2 * NT])
        result_i = sb("result_i", [P, S, 2 * NT], U32)

        xt = sb("xt", [P, 2, HID])
        xtT = sb("xtT", [P, ROWS])
        sil = kJ[:].rearrange("p n a j -> p (n a j)")[:, 0:FB * ROWS].rearrange("p (f n) -> p f n", f=FB)
        hT = vJ[:].rearrange("p n a j -> p (n a j)")[:, 0:FB * ROWS].rearrange("p (f n) -> p f n", f=FB)
        y = sb("y", [P, 2, HID])
        cx = sb("cx", [P, NT, HID])
        cidx = sb("cidx", [P, 2 * NT], U32)
        cgate = sb("cgate", [P, 2, NT])
        cy = S_mid[:].rearrange("p n a j -> p (n a j)")[:, 0:2 * NT * HID].rearrange("p (k t h) -> p k t h", k=2, t=NT)
        cf = sb("cf", [P, NT, HID])
        cn = sb("cn", [P, NT, HID])
        co = sb("co", [P, NT, HID])

        pA = [ps(f"pA{n}", [P, PAIRS, R * C]) for n in range(2)]
        pO = [ps(f"pO{n}", [P, 4, P]) for n in range(2)]
        pJ = [ps(f"pJ{n}", [P, 512]) for n in range(2)]
        pT = ps("pT", [P, 512])
        pW = ps("pW", [P, 512])

        block = ctx.enter_context(nc.Block())
        settled = sem("settled")
        rows_free = sem("rows_free")
        vJ_zero = sem("vJ_zero")
        weights_in = sem("weights_in")
        const_made = sem("const_made")
        xa_in = sem("xa_in")
        xr_in = sem("xr_in")
        x1_out = sem("x1_out")
        xn_stat = sem("xn_stat")
        xn_rstd = sem("xn_rstd")
        xn_lnv = sem("xn_lnv")
        xn_ready = sem("xn_ready")
        xnT_psum = sem("xnT_psum")
        xnT_ready = sem("xnT_ready")
        h1_psum = sem("h1_psum")
        h1_ready = sem("h1_ready")
        z_psum = sem("z_psum")
        absz_ready = sem("absz_ready")
        minz_ready = sem("minz_ready")
        ez_ready = sem("ez_ready")
        lz_ready = sem("lz_ready")
        gate_ready = sem("gate_ready")
        run_ready = sem("run_ready")
        rel_ready = sem("rel_ready")
        steplog_ready = sem("steplog_ready")
        decay_ready = sem("decay_ready")
        step_ready = sem("step_ready")
        k_psum = sem("k_psum")
        k_ready = sem("k_ready")
        v_psum = sem("v_psum")
        v_ready = sem("v_ready")
        q_psum = sem("q_psum")
        q_ready = sem("q_ready")
        kJ_psum = sem("kJ_psum")
        kJ_ready = sem("kJ_ready")
        upd_psum = sem("upd_psum")
        raw_ready = sem("raw_ready")
        mid_ready = sem("mid_ready")
        a_psum = sem("a_psum")
        a_ready = sem("a_ready")
        o_psum = sem("o_psum")
        sq_ready = sem("sq_ready")
        ss_ready = sem("ss_ready")
        lnss_ready = sem("lnss_ready")
        rs_ready = sem("rs_ready")
        on_ready = sem("on_ready")
        ot_psum = sem("ot_psum")
        ot_ready = sem("ot_ready")
        w_psum = sem("w_psum")
        w_stat = sem("w_stat")
        w_lnv = sem("w_lnv")
        w_rstd = sem("w_rstd")
        an_ready = sem("an_ready")
        x1_ready = sem("x1_ready")
        r_stat = sem("r_stat")
        r_aggr = sem("r_aggr")
        r_lnv = sem("r_lnv")
        r_rstd = sem("r_rstd")
        x1n_ready = sem("x1n_ready")
        x1nT_psum = sem("x1nT_psum")
        x1nT_ready = sem("x1nT_ready")
        logit_psum = sem("logit_psum")
        logit_ready = sem("logit_ready")
        top_ready = sem("top_ready")
        topi_ready = sem("topi_ready")
        topf_ready = sem("topf_ready")
        pick_ready = sem("pick_ready")
        both_ready = sem("both_ready")
        rank_psum = sem("rank_psum")
        place_ready = sem("place_ready")
        base_ready = sem("base_ready")
        placed_ready = sem("placed_ready")
        rowf_ready = sem("rowf_ready")
        rowi_ready = sem("rowi_ready")
        diff_ready = sem("diff_ready")
        ediff_ready = sem("ediff_ready")
        den_ready = sem("den_ready")
        g1_ready = sem("g1_ready")
        g2_ready = sem("g2_ready")
        kept = sem("kept")
        scattered = sem("scattered")
        dve_step = sem("dve_step")
        counts_ready = sem("counts_ready")
        tail_in = sem("tail_in")
        pad_out = sem("pad_out")
        xt_in = sem("xt_in")
        xt_psum = sem("xt_psum")
        xt_ready = sem("xt_ready")
        up_psum = sem("up_psum")
        silu_ready = sem("silu_ready")
        h_ready = sem("h_ready")
        y_psum = sem("y_psum")
        y_ready = sem("y_ready")
        y_out = sem("y_out")
        c_x1 = sem("c_x1")
        c_idx = sem("c_idx")
        c_gath = sem("c_gath")
        c_mul = sem("c_mul")
        c_sum = sem("c_sum")
        c_stat = sem("c_stat")
        c_lnv = sem("c_lnv")
        c_rstd = sem("c_rstd")
        c_norm = sem("c_norm")
        c_res = sem("c_res")
        c_out = sem("c_out")

        FIRST = 1

        def settle(eng):
            eng.sem_inc(settled, 1)

        xv = x.rearrange("s (t p) h -> s p t h", p=P)
        x1v = x1_dram.rearrange("(s t p) h -> s p t h", p=P, t=NT)
        ov = out.rearrange("s (t p) h -> s p t h", p=P)

        def seq(v, i):
            return v[bass.ds(i, 1)].rearrange("a p t h -> p (a t) h")

        def wide(ap, *shape):
            return ap.to_broadcast(list(shape))

        WEIGHTS = [(wq_sb, wq), (wk_sb, wk), (wv_sb, wv), (wo_sb, wo), (wg1_sb, wg1), (wg2_sb, wg2),
                   (bg2_sb, bg2), (gn_sb, gnorm), (rw_sb, rw), (rb_sb, rb.to_broadcast([P, E])), (cst, consts)]
        BIG = [(wgate_sb, wgate), (wup_sb, wup), (wdown_sb, wdown)]

        @block.sync
        def _(sp):
            for credited in (x1_ready, x1nT_ready, base_ready, x1_out, x1n_ready, rows_free, h_ready,
                             y_ready, y_out, y_psum, c_res, c_out, c_sum):
                sp.sem_inc(credited, FIRST)
            sp.dma_start(xa[:], seq(xv, 0)).then_inc(xa_in, 16)
            for dst, src in WEIGHTS:
                sp.dma_start(dst[:], src).then_inc(weights_in, 16)
            for dst, src in BIG:
                sp.dma_start(dst[:], src).then_inc(tail_in, 16)

            def sequence(i, more):
                if more:
                    sp.wait_ge(xn_ready, (i + 1) * NT)
                    settle(sp)
                    sp.dma_start(xa[:], seq(xv, i + 1)).then_inc(xa_in, 16)
                sp.wait_ge(x1_ready, FIRST + i * NT)
                settle(sp)
                sp.dma_start(xr[:], seq(xv, i)).then_inc(xr_in, 16)
                sp.wait_ge(x1_ready, FIRST + (i + 1) * NT)
                settle(sp)
                sp.dma_start(seq(x1v, i), x1[:]).then_inc(x1_out, 16)

            with sp.Fori(0, S - 1) as i:
                sequence(i, True)
            sequence(S - 1, False)

            zero_rows = zeros[:].rearrange("p (t h) -> p t h", h=HID)
            for t in range(2 * T // ROWS, TILES):
                sp.dma_start(ys_dram[t * ROWS:t * ROWS + ROWS].rearrange("(t p) h -> p t h", p=P),
                             zero_rows).then_inc(pad_out, 16)
            sp.wait_ge(counts_ready, 1)
            for e in range(E):
                first = sp.value_load(end_i[0:1, e:e + 1], min_val=e * CAP, max_val=e * CAP + T)
                sp.dma_start(xs_dram[bass.ds(first, ROWS)].rearrange("(t p) h -> p t h", p=P),
                             zero_rows).then_inc(pad_out, 16)
            sp.dma_start(xs_dram[E * CAP:E * CAP + ROWS].rearrange("(t p) h -> p t h", p=P),
                         zero_rows).then_inc(pad_out, 16)
            sp.wait_ge(pad_out, 16 * (E + 1 + TILES - 2 * T // ROWS))
            sp.wait_ge(scattered, 16 * 2 * NT * S)

            def load_tile(t):
                first = sp.value_load(trow_i[0:1, bass.ds(t, 1)], min_val=0, max_val=E * CAP)
                sp.dma_start(xt[:], xs_dram[bass.ds(first, ROWS)].rearrange("(t p) h -> p t h", p=P))\
                  .then_inc(xt_in, 16)
                return first

            load_tile(0)
            total = sp.value_load(cum_i[0:1, E - 1:E], min_val=E, max_val=TILES)
            with sp.Fori(0, total) as t:
                sp.wait_ge(xt_psum, t + 1)
                settle(sp)
                load_tile(t + 1)
            sp.wait_ge(xt_in, total * 16 + 16)
            settle(sp)

            with sp.Fori(0, S) as i:
                sp.wait_ge(c_res, FIRST + i)
                settle(sp)
                sp.dma_start(cx[:], seq(x1v, i)).then_inc(c_x1, 16)
                sp.wait_ge(c_res, FIRST + i + 1)
                settle(sp)
                sp.dma_start(seq(ov, i), co[:]).then_inc(c_out, 16)
                sp.wait_ge(c_out, FIRST + i * 16 + 16)
                settle(sp)

        @block.tensor
        def _(pe):
            mm, tr = nc.tensor.matmul, nc.tensor.transpose

            def norm_transposes(j):
                pe.wait_ge(xn_ready, j * NT + NT)
                for t in range(NT):
                    last = tr(pT[:, t * P:(t + 1) * P], xn[:, t, :], ident)
                last.then_inc(xnT_psum, 1)

            def gate_low(j):
                pe.wait_ge(xnT_ready, j * 2 + 2)
                pe.wait_ge(raw_ready, j * (NC - 1))
                mm(pJ[0][0:LOW, :], wg1_sb[:], xnT[:, :, 0, :], start=True, stop=True).then_inc(h1_psum, 1)

            def gate_high(j):
                pe.wait_ge(h1_ready, j + 1)
                for p in range(PAIRS):
                    mm(pJ[p][:], wg2_sb[:, p, :], h1[:], start=True, stop=True).then_inc(z_psum, 1)

            def project(j):
                pe.wait_ge(absz_ready, j * 2 + 2)
                pe.wait_ge(minz_ready, j * 2 + 2)
                for p in range(PAIRS):
                    mm(pJ[p][:], wk_sb[:, p, :], xnT[:, :, 0, :], start=True, stop=True).then_inc(k_psum, 1)
                for g in range(NC // 2):
                    if g < 2:
                        pe.wait_ge(k_ready, j * 4 + 2 * g + 2)
                    else:
                        pe.wait_ge(v_ready, j * NC + 2 * (g - 1))
                    for c in (2 * g, 2 * g + 1):
                        last = mm(pJ[g % 2][:, (c % 2) * 256:(c % 2) * 256 + 256],
                                  xnT[:, c, :, :].rearrange("p a c -> p (a c)"), wv_sb[:], start=True, stop=True)
                    last.then_inc(v_psum, 1)
                for b in range(PAIRS * R):
                    if b < 2:
                        pe.wait_ge(v_ready, j * NC + 2 * (b + 3))
                    else:
                        pe.wait_ge(q_ready, j * 8 + b - 1)
                    mm(pJ[b % 2][:], wq_sb[:, b // R, b % R, :], xnT[:, :, 0, :],
                       start=True, stop=True).then_inc(q_psum, 1)

            def key_transposes(j):
                pe.wait_ge(k_ready, j * 4 + 4)
                for g in range(NC // 2):
                    if g > 0:
                        pe.wait_ge(kJ_ready, j * 4 + g)
                    for c in range(2 * g, min(2 * g + 2, NC - 1)):
                        for p in range(PAIRS):
                            last = tr(pT[:, ((c % 2) * 2 + p) * P:((c % 2) * 2 + p + 1) * P], kT[:, p, c, :], ident)
                    last.then_inc(kJ_psum, 1)

            def state_updates(j):
                for c in range(NC - 1):
                    pe.wait_ge(kJ_ready, j * 4 + c // 2 + 1)
                    if c < 2:
                        pe.wait_ge(q_ready, j * 8 + 7 + c)
                    else:
                        pe.wait_ge(raw_ready, j * (NC - 1) + c - 1)
                    for p in range(PAIRS):
                        last = mm(pJ[c % 2][:, p * P:(p + 1) * P], kJ[:, c, p, :], vJ[:, c, p, :],
                                  start=True, stop=True)
                    last.then_inc(upd_psum, 1)

            def scores(i, c):
                pe.wait_ge(q_ready, i * 8 + 8)
                if c >= 2:
                    pe.wait_ge(a_ready, i * NC + c - 1)
                for p in range(PAIRS):
                    last = mm(pA[c % 2][:, p, :], kT[:, p, c, :],
                              qT[:, p, c, :, :].rearrange("p r c -> p (r c)"), start=True, stop=True)
                last.then_inc(a_psum, 1)

            def outputs(i, c):
                pe.wait_ge(a_ready, i * NC + c + 1)
                if c >= 2:
                    pe.wait_ge(on_ready, i * NC + c - 1)
                if c > 0:
                    pe.wait_ge(mid_ready, i * (NC - 1) + c)
                for p in range(PAIRS):
                    for h in range(2):
                        o = pO[c % 2][:, 2 * p + h, :]
                        last = mm(o, aT[:, c % 2, p, h * P:(h + 1) * P], vJ[:, c, p, :], start=True, stop=(c == 0))
                        if c > 0:
                            last = mm(o, qT[:, p, c, 2 * h:2 * h + 2, :].rearrange("p r c -> p (r c)"),
                                      S_mid[:, c, p, :], start=False, stop=True)
                last.then_inc(o_psum, 1)

            def out_transposes(i, c, after_norm=False):
                pe.wait_ge(on_ready, i * NC + c + 1)
                if after_norm:
                    pe.wait_ge(xnT_ready, i * 2 + 4)
                elif c > 0:
                    pe.wait_ge(ot_ready, i * NC + c)
                else:
                    pe.wait_ge(x1nT_ready, FIRST + i)
                for k in range(4):
                    last = tr(pT[:, k * P:(k + 1) * P], on[:, c % 2, k, :], ident)
                last.then_inc(ot_psum, 1)

            def merge_heads(i, t):
                pe.wait_ge(ot_ready, i * NC + 2 * t + 2)
                if t > 0:
                    pe.wait_ge(an_ready, i * NT + t)
                else:
                    pe.wait_ge(base_ready, FIRST + i)
                for b in range(PAIRS * R):
                    last = mm(pW[:, 0:HID], oT[:, t % 2, b, :, :].rearrange("p a c -> p (a c)"), wo_sb[:, b, :],
                              start=(b == 0), stop=(b == PAIRS * R - 1))
                last.then_inc(w_psum, 1)

            def chunks(i, more):
                scores(i, 0)
                for c in range(NC):
                    if c + 1 < NC:
                        scores(i, c + 1)
                    outputs(i, c)
                    if c > 0:
                        out_transposes(i, c - 1, after_norm=(more and c == 5))
                    if c in (3, 5, 7):
                        merge_heads(i, (c - 3) // 2)
                    if more and c == 4:
                        pe.wait_ge(ot_ready, i * NC + c)
                        norm_transposes(i + 1)
                    if more and c == 5:
                        gate_low(i + 1)
                    if more and c == 6:
                        gate_high(i + 1)

            def route(i):
                pe.wait_ge(x1n_ready, FIRST + i * NT + NT)
                pe.wait_ge(an_ready, i * NT + NT)
                for t in range(NT):
                    last = tr(pT[:, t * P:(t + 1) * P], x1n[:, t, :], ident)
                last.then_inc(x1nT_psum, 1)
                pe.wait_ge(x1nT_ready, FIRST + i + 1)
                for t in range(NT):
                    last = mm(pW[:, t * E:(t + 1) * E], x1nT[:, t, :], rw_sb[:], start=True, stop=True)
                last.then_inc(logit_psum, 1)
                pe.wait_ge(both_ready, i + 1)
                for t in range(NT + 1):
                    o = pW[:, t * E:(t + 1) * E]
                    for u in range(min(t, NT)):
                        last = mm(o, ones[:], both[:, u, :], start=(u == 0), stop=(t == NT and u == NT - 1))
                    if t < NT:
                        last = mm(o, tri[:], both[:, t, :], start=(t == 0), stop=True)
                last.then_inc(rank_psum, 1)

            pe.wait_ge(weights_in, 16 * len(WEIGHTS))
            pe.wait_ge(const_made, 5)
            norm_transposes(0)
            gate_low(0)
            gate_high(0)
            project(0)
            key_transposes(0)
            state_updates(0)
            with pe.Fori(0, S - 1) as i:
                chunks(i, True)
                out_transposes(i, NC - 1)
                project(i + 1)
                merge_heads(i, NT - 1)
                key_transposes(i + 1)
                state_updates(i + 1)
                route(i)
            chunks(S - 1, False)
            out_transposes(S - 1, NC - 1)
            merge_heads(S - 1, NT - 1)
            route(S - 1)

            def rows_transposed(t):
                pe.wait_ge(xt_in, t * 16 + 16)
                for k in range(2):
                    last = tr(pT[:, k * P:(k + 1) * P], xt[:, k, :], ident)
                last.then_inc(xt_psum, 1)

            pe.wait_ge(tail_in, 16 * len(BIG))
            pe.wait_ge(counts_ready, 1)
            bank = [pA[0][:].rearrange("p a c -> p (a c)"), pA[1][:].rearrange("p a c -> p (a c)"),
                    pJ[0][:], pJ[1][:]]
            ybank = [pO[0][:, 0, :], pO[1][:, 0, :]]
            rows_transposed(0)
            ends = [pe.value_load(cum_i[0:1, e:e + 1], min_val=e + 1, max_val=TILES) for e in range(E)]
            for e in range(E):
                with pe.Fori(0 if e == 0 else ends[e - 1], ends[e]) as t:
                    pe.wait_ge(xt_ready, t + 1)
                    for f in range(FB):
                        pe.wait_ge(h_ready, FIRST + t * FB)
                        mm(bank[f][:, 0:ROWS], wgate_sb[:, e, f * P:(f + 1) * P], xtT[:], start=True, stop=True)
                        mm(bank[f][:, ROWS:2 * ROWS], wup_sb[:, e, f * P:(f + 1) * P], xtT[:],
                           start=True, stop=True).then_inc(up_psum, 1)
                    rows_transposed(t + 1)
                    pe.wait_ge(y_ready, FIRST + t * 2)
                    for f in range(FB):
                        pe.wait_ge(h_ready, FIRST + t * FB + f + 1)
                        for k in range(2):
                            last = mm(ybank[k], hT[:, f, k * P:(k + 1) * P], wdown_sb[:, e, f, :],
                                      start=(f == 0), stop=(f == FB - 1))
                    last.then_inc(y_psum, 1)

        @block.scalar
        def _(act):
            a = nc.scalar.activation

            def eps(col):
                return cst[:, col:col + 1]

            def norm_rstd(j):
                act.wait_ge(xn_stat, j * 2 * NT + 2 * NT)
                a(lnv[:, 0, :], mv[:, 0, :, 1], ACT.Ln, bias=eps(C_EPS_LN)).then_inc(xn_lnv, 1)
                act.wait_ge(xn_lnv, j + 1)
                a(rstd[:, 0, :], lnv[:, 0, :], ACT.Exp, scale=-0.5).then_inc(xn_rstd, 1)

            def norm_T(j):
                act.wait_ge(xnT_psum, j + 1)
                for k in range(2):
                    a(xnT[:, :, k, :], pT[:].rearrange("p (n c) -> p n c", c=C), ACT.Copy)\
                        .then_inc(xnT_ready, 1)

            def gates(j):
                act.wait_ge(gate_ready, j)
                for p in range(PAIRS):
                    act.wait_ge(z_psum, j * 2 + p + 1)
                    a(absz[:, p, :], pJ[p][:], ACT.Abs, bias=bg2_sb[:, p:p + 1]).then_inc(absz_ready, 1)
                act.wait_ge(absz_ready, j * 2 + 2)
                a(absz[:], absz[:], ACT.Exp, scale=-1.0).then_inc(ez_ready, 1)
                act.wait_ge(ez_ready, j + 1)
                a(absz[:], absz[:], ACT.Ln, bias=1.0).then_inc(lz_ready, 1)

            def decays(j):
                act.wait_ge(rel_ready, j + 1)
                a(grow[:], rel[:], ACT.Exp, scale=1.0 / GATE_NORMALIZER).then_inc(decay_ready, 1)
                a(shrink[:], rel[:], ACT.Exp, scale=-1.0 / GATE_NORMALIZER).then_inc(decay_ready, 1)
                act.wait_ge(steplog_ready, j + 1)
                a(step[:, :, 0:NC - 1], step_log[:, :, 0:NC - 1], ACT.Exp,
                  scale=1.0 / GATE_NORMALIZER).then_inc(step_ready, 1)

            def values(j):
                for g in range(NC // 2):
                    act.wait_ge(v_psum, j * 4 + g + 1)
                    for half in range(2):
                        rows = slice(half * D, half * D + D)
                        a(vJ[rows, 2 * g:2 * g + 2, :, half * D:half * D + D].rearrange("p c q d -> p (c q) d"),
                          pJ[g % 2][rows, :].rearrange("p (n h d) -> p n h d", h=2, d=D)[:, :, half, :],
                          ACT.Copy).then_inc(v_ready, 1)

            def keys(j):
                for g in range(NC // 2):
                    act.wait_ge(kJ_psum, j * 4 + g + 1)
                    n = min(2, NC - 1 - 2 * g)
                    a(kJ[:, 2 * g:2 * g + n, :, :].rearrange("p c q j -> p (c q j)"), pT[:, 0:n * 2 * P],
                      ACT.Copy).then_inc(kJ_ready, 1)

            def head_norm(i, c):
                act.wait_ge(o_psum, i * NC + c + 1)
                a(sq[:, c % 2, :], pO[c % 2][:].rearrange("p k v -> p (k v)"), ACT.Square)\
                    .then_inc(sq_ready, 1)
                act.wait_ge(ss_ready, i * NC + c + 1)
                a(lnss[:, c % 2, :], ss[:, c % 2, :], ACT.Ln, scale=1.0 / D, bias=eps(C_EPS_HEAD))\
                    .then_inc(lnss_ready, 1)
                act.wait_ge(lnss_ready, i * NC + c + 1)
                a(rs[:, c % 2, :], lnss[:, c % 2, :], ACT.Exp, scale=-0.5).then_inc(rs_ready, 1)

            def out_T(i, c):
                act.wait_ge(ot_psum, i * NC + c + 1)
                a(oT[:, (c // 2) % 2, :, c % 2, :], pT[:].rearrange("p (b c) -> p b c", c=C), ACT.Copy,
                  scale=gn_sb[:, 0:1]).then_inc(ot_ready, 1)

            def merged_rstd(i, t):
                act.wait_ge(w_stat, (i * NT + t) * 2 + 2)
                a(lnv[:, 1, t:t + 1], mv[:, 1, t, 1:2], ACT.Ln, bias=eps(C_EPS_LN)).then_inc(w_lnv, 1)
                act.wait_ge(w_lnv, i * NT + t + 1)
                a(rstd[:, 1, t:t + 1], lnv[:, 1, t:t + 1], ACT.Exp, scale=-0.5).then_inc(w_rstd, 1)

            def chunks(i, more):
                for c in range(NC):
                    head_norm(i, c)
                    if c > 0:
                        out_T(i, c - 1)
                    if c in (3, 5, 7):
                        merged_rstd(i, (c - 3) // 2)
                    if more and c == 2:
                        norm_rstd(i + 1)
                    if more and c == 4:
                        norm_T(i + 1)
                    if more and c == 6:
                        gates(i + 1)
                out_T(i, NC - 1)
                if more:
                    decays(i + 1)

            def route(i):
                act.wait_ge(r_aggr, i * NT + NT)
                a(lnv[:, 2, :], mv[:, 2, :, 1], ACT.Ln, bias=eps(C_EPS_LN)).then_inc(r_lnv, 1)
                act.wait_ge(r_lnv, i + 1)
                a(rstd[:, 2, :], lnv[:, 2, :], ACT.Exp, scale=-0.5).then_inc(r_rstd, 1)
                act.wait_ge(x1nT_psum, i + 1)
                a(x1nT[:].rearrange("p t j -> p (t j)"), pT[:], ACT.Copy).then_inc(x1nT_ready, 1)
                act.wait_ge(diff_ready, i + 1)
                a(ediff[:], diff[:], ACT.Exp).then_inc(ediff_ready, 1)

            act.wait_ge(weights_in, 16 * len(WEIGHTS))
            act.wait_ge(vJ_zero, 1)
            act.preload_act_table_set(LOG_EXP)
            norm_rstd(0)
            norm_T(0)
            gates(0)
            decays(0)
            values(0)
            keys(0)
            with act.Fori(0, S - 1) as i:
                act.preload_act_table_set(LOG_EXP)
                chunks(i, True)
                values(i + 1)
                merged_rstd(i, NT - 1)
                keys(i + 1)
                route(i)
            act.preload_act_table_set(LOG_EXP)
            chunks(S - 1, False)
            merged_rstd(S - 1, NT - 1)
            route(S - 1)

            act.wait_ge(counts_ready, 1)
            total = act.value_load(cum_i[0:1, E - 1:E], min_val=E, max_val=TILES)
            bank = [pA[0][:].rearrange("p a c -> p (a c)"), pA[1][:].rearrange("p a c -> p (a c)"),
                    pJ[0][:], pJ[1][:]]
            act.wait_ge(xt_psum, 1)
            a(xtT[:], pT[:, 0:ROWS], ACT.Copy).then_inc(xt_ready, 1)
            with act.Fori(0, total) as t:
                for f in range(FB):
                    act.wait_ge(up_psum, t * FB + f + 1)
                    act.wait_ge(h_ready, FIRST + t * FB)
                    a(sil[:, f, :], bank[f][:, 0:ROWS], ACT.Silu).then_inc(silu_ready, 1)
                act.wait_ge(xt_psum, t + 2)
                a(xtT[:], pT[:, 0:ROWS], ACT.Copy).then_inc(xt_ready, 1)
                act.wait_ge(y_psum, FIRST + t + 1)
                act.wait_ge(y_out, FIRST + t * 16)
                a(y[:, 0, :], pO[0][:, 0, :], ACT.Copy).then_inc(y_ready, 1)
                a(y[:, 1, :], pO[1][:, 0, :], ACT.Copy).then_inc(y_ready, 1)
                act.wait_ge(y_ready, FIRST + t * 2 + 2)
                act.dma_start(ys_dram[bass.ds(t * ROWS, ROWS)].rearrange("(t p) h -> p t h", p=P), y[:])\
                   .then_inc(y_out, 16)
            act.wait_ge(y_out, FIRST + total * 16)

            with act.Fori(0, S) as i:
                act.preload_act_table_set(LOG_EXP)
                act.wait_ge(c_stat, i * 2 * NT + 2 * NT)
                a(lnv[:, 0, :], mv[:, 0, :, 1], ACT.Ln, bias=eps(C_EPS_LN)).then_inc(c_lnv, 1)
                act.wait_ge(c_lnv, i + 1)
                a(rstd[:, 0, :], lnv[:, 0, :], ACT.Exp, scale=-0.5).then_inc(c_rstd, 1)

        @block.vector
        def _(dve):
            v = nc.vector

            def norm_stats(j):
                dve.wait_ge(xa_in, j * 16 + 16)
                for t in range(NT):
                    v.bn_stats(st[:, 0, t, :], xa[:, t, :]).then_inc(xn_stat, 1)
                dve.wait_ge(xn_stat, j * 2 * NT + NT)
                settle(dve)
                for t in range(NT):
                    v.bn_aggr(mv[:, 0, t, :], st[:, 0, t, :]).then_inc(xn_stat, 1)

            def norm_apply(j):
                dve.wait_ge(xn_rstd, j + 1)
                for t in range(NT):
                    v.tensor_scalar(xn[:, t, :], xa[:, t, :], mv[:, 0, t, 0:1], rstd[:, 0, t:t + 1],
                                    ALU.subtract, ALU.mult).then_inc(xn_ready, 1)

            def gate_copy(j):
                dve.wait_ge(h1_psum, j + 1)
                v.tensor_copy(h1[:], pJ[0][0:LOW, :]).then_inc(h1_ready, 1)

            def gate_min(j):
                for p in range(PAIRS):
                    dve.wait_ge(absz_ready, j * 2 + p + 1)
                    v.tensor_scalar(minz[:, p, :], pJ[p][:], bg2_sb[:, p:p + 1], 0.0, ALU.add, ALU.min)\
                        .then_inc(minz_ready, 1)

            def gate_sums(j):
                dve.wait_ge(lz_ready, j + 1)
                dve.wait_ge(minz_ready, j * 2 + 2)
                v.tensor_tensor(minz[:], minz[:], absz[:], ALU.subtract).then_inc(gate_ready, 1)
                dve.wait_ge(gate_ready, j + 1)
                v.tensor_tensor_scan(run[:].rearrange("p a l -> p (a l)"), in_chunk,
                                     minz[:].rearrange("p a l -> p (a l)"), 0.0, ALU.mult, ALU.add)\
                    .then_inc(run_ready, 1)
                dve.wait_ge(run_ready, j + 1)
                r4 = run[:].rearrange("p a (n c) -> p (a n) c", c=C)
                mid = C // 2 - 1
                v.tensor_tensor(rel[:].rearrange("p a (n c) -> p (a n) c", c=C), r4,
                                wide(r4[:, :, mid:mid + 1], P, PAIRS * NC, C), ALU.subtract)\
                    .then_inc(rel_ready, 1)
                dve.wait_ge(rel_ready, j + 1)
                rn = run[:].rearrange("p a (n c) -> p a n c", c=C)
                ln = rel[:].rearrange("p a (n c) -> p a n c", c=C)
                v.tensor_tensor(step_log[:, :, 0:NC - 1], ln[:, :, 0:NC - 1, C - 1], rn[:, :, 1:NC, mid], ALU.add)\
                    .then_inc(steplog_ready, 1)

            def keys(j):
                dve.wait_ge(decay_ready, j * 2 + 2)
                for p in range(PAIRS):
                    dve.wait_ge(k_psum, j * 2 + p + 1)
                    for half in range(2):
                        rows = slice(half * D, half * D + D)
                        v.scalar_tensor_tensor(
                            out=kT[rows, p, :, half * C:half * C + C],
                            in0=pJ[p][rows, :].rearrange("p (n c) -> p n c", c=C), scalar=0.0,
                            in1=shrink[rows, p, :].rearrange("p (n c) -> p n c", c=C),
                            op0=ALU.max, op1=ALU.mult).then_inc(k_ready, 1)

            def queries(j):
                for b in range(PAIRS * R):
                    dve.wait_ge(q_psum, j * 8 + b + 1)
                    v.scalar_tensor_tensor(
                        out=qT[:, b // R, :, b % R, :], in0=pJ[b % 2][:].rearrange("p (n c) -> p n c", c=C),
                        scalar=0.0, in1=grow[:, b // R, :].rearrange("p (n c) -> p n c", c=C),
                        op0=ALU.max, op1=ALU.mult).then_inc(q_ready, 1)

            def states(j):
                dve.wait_ge(step_ready, j + 1)
                for c in range(NC - 1):
                    dve.wait_ge(upd_psum, j * (NC - 1) + c + 1)
                    u = pJ[c % 2][:, 0:2 * P].rearrange("p (a v) -> p a v", a=PAIRS)
                    if c >= 2:
                        dve.wait_ge(mid_ready, j * (NC - 1) + c - 1)
                    if c == 0:
                        v.tensor_copy(S_raw[:, 0, :, :], u).then_inc(raw_ready, 1)
                    else:
                        dve.wait_ge(raw_ready, j * (NC - 1) + c)
                        for p in range(PAIRS):
                            ins = v.scalar_tensor_tensor(
                                out=S_raw[:, c % 2, p, :], in0=S_raw[:, (c - 1) % 2, p, :],
                                scalar=step[:, p, c - 1:c], in1=u[:, p, :], op0=ALU.mult, op1=ALU.add)
                        ins.then_inc(raw_ready, 1)

            def mask(i, c):
                dve.wait_ge(a_psum, i * NC + c + 1)
                v.tensor_tensor(
                    aT[:, c % 2, :, :].rearrange("p a (r c) -> p (a r) c", c=C),
                    pA[c % 2][:].rearrange("p a (r c) -> p (a r) c", c=C),
                    wide(causal.unsqueeze(1), P, PAIRS * R, C), ALU.mult).then_inc(a_ready, 1)

            def head_norm(i, c):
                dve.wait_ge(sq_ready, i * NC + c + 1)
                v.tensor_reduce(ss[:, c % 2, :], sq[:, c % 2, :].rearrange("p (n d) -> p n d", d=D), AX, ALU.add)\
                    .then_inc(ss_ready, 1)
                dve.wait_ge(rs_ready, i * NC + c + 1)
                v.tensor_tensor(
                    on[:, c % 2, :, :].rearrange("p k (h d) -> p (k h) d", d=D),
                    pO[c % 2][:].rearrange("p k (h d) -> p (k h) d", d=D),
                    wide(rs[:, c % 2, :].unsqueeze(2), P, 8, D), ALU.mult).then_inc(on_ready, 1)

            def merged(i, t):
                n = i * NT + t
                dve.wait_ge(w_psum, n + 1)
                v.bn_stats(st[:, 1, t, :], pW[:, 0:HID]).then_inc(w_stat, 1)
                dve.wait_ge(w_stat, n * 2 + 1)
                settle(dve)
                v.bn_aggr(mv[:, 1, t, :], st[:, 1, t, :]).then_inc(w_stat, 1)
                dve.wait_ge(w_rstd, n + 1)
                dve.wait_ge(x1_ready, FIRST + i * NT)
                v.tensor_scalar(an[:, t, :], pW[:, 0:HID], mv[:, 1, t, 0:1], rstd[:, 1, t:t + 1],
                                ALU.subtract, ALU.mult).then_inc(an_ready, 1)

            def chunks(i, more):
                mask(i, 0)
                for c in range(NC):
                    if c + 1 < NC:
                        mask(i, c + 1)
                    head_norm(i, c)
                    if c in (3, 5, 7):
                        merged(i, (c - 3) // 2)
                    if more and c == 1:
                        norm_stats(i + 1)
                    if more and c == 2:
                        norm_apply(i + 1)
                    if more and c == 5:
                        gate_copy(i + 1)
                    if more and c == 6:
                        gate_min(i + 1)
                if more:
                    dve.wait_ge(mid_ready, i * (NC - 1) + NC - 1)
                    gate_sums(i + 1)

            def route(i):
                dve.wait_ge(x1_ready, FIRST + i * NT + NT)
                for t in range(NT):
                    v.bn_stats(st[:, 2, t, :], x1[:, t, :]).then_inc(r_stat, 1)
                dve.wait_ge(r_stat, i * NT + NT)
                settle(dve)
                for t in range(NT):
                    v.bn_aggr(mv[:, 2, t, :], st[:, 2, t, :]).then_inc(r_aggr, 1)
                dve.wait_ge(r_rstd, i + 1)
                dve.wait_ge(rows_free, FIRST + i)
                for t in range(NT):
                    v.tensor_scalar(x1n[:, t, :], x1[:, t, :], mv[:, 2, t, 0:1], rstd[:, 2, t:t + 1],
                                    ALU.subtract, ALU.mult).then_inc(x1n_ready, 1)
                dve.wait_ge(logit_psum, i + 1)
                v.tensor_tensor(logit[:], pW[:, 0:NT * E].rearrange("p (t e) -> p t e", e=E),
                                wide(rb_sb[:].unsqueeze(1), P, NT, E), ALU.add).then_inc(logit_ready, 1)
                dve.wait_ge(logit_ready, i + 1)
                settle(dve)
                for t in range(NT):
                    v.max(top[:, t, :], logit[:, t, :]).then_inc(top_ready, 1)
                dve.wait_ge(top_ready, i * NT + NT)
                settle(dve)
                for t in range(NT):
                    v.max_index(top_i[:, t, :], top[:, t, :], logit[:, t, :]).then_inc(topi_ready, 1)
                v.tensor_tensor(diff[:], top[:, :, 1], top[:, :, 0], ALU.subtract).then_inc(diff_ready, 1)
                dve.wait_ge(topi_ready, i * NT + NT)
                v.tensor_copy(top_f[:], top_i[:]).then_inc(topf_ready, 1)
                dve.wait_ge(topf_ready, i + 1)
                for k in range(2):
                    v.tensor_tensor(pick[:, k, :, :], wide(iota8.unsqueeze(1), P, NT, E),
                                    wide(top_f[:, :, k:k + 1], P, NT, E), ALU.is_equal).then_inc(pick_ready, 1)
                dve.wait_ge(pick_ready, i * 2 + 2)
                v.tensor_tensor(both[:], pick[:, 0, :, :], pick[:, 1, :, :], ALU.add).then_inc(both_ready, 1)
                dve.wait_ge(ediff_ready, i + 1)
                v.tensor_scalar(den[:], ediff[:], 1.0, None, ALU.add).then_inc(den_ready, 1)
                dve.wait_ge(den_ready, i + 1)
                v.reciprocal(gts[:, 0, :], den[:]).then_inc(g1_ready, 1)
                dve.wait_ge(g1_ready, i + 1)
                v.tensor_tensor(gts[:, 1, :], gts[:, 0, :], ediff[:], ALU.mult).then_inc(g2_ready, 1)
                dve.wait_ge(rank_psum, i + 1)
                dve.wait_ge(base_ready, FIRST + i)
                v.tensor_tensor(place[:], pW[:, 0:NT * E].rearrange("p (t e) -> p t e", e=E),
                                wide(base[:].unsqueeze(1), P, NT, E), ALU.add).then_inc(place_ready, 1)
                dve.wait_ge(place_ready, i + 1)
                v.tensor_tensor(base[:], base[:], pW[:, NT * E:(NT + 1) * E], ALU.add).then_inc(base_ready, 1)
                v.tensor_tensor(placed[:], pick[:], wide(place[:].unsqueeze(1), P, 2, NT, E), ALU.mult)\
                    .then_inc(placed_ready, 1)
                dve.wait_ge(placed_ready, i + 1)
                v.tensor_reduce(rowf[:], placed[:], AX, ALU.add).then_inc(rowf_ready, 1)
                dve.wait_ge(rowf_ready, i + 1)
                v.tensor_copy(rowi[:], rowf[:]).then_inc(rowi_ready, 1)
                dve.wait_ge(rowi_ready, i + 1)
                dve.wait_ge(g2_ready, i + 1)
                v.tensor_copy(rows_all[:, bass.ds(i, 1), :].rearrange("p a n -> p (a n)"),
                              rowf[:].rearrange("p k t -> p (k t)")).then_inc(kept, 1)
                for k in range(2):
                    v.tensor_copy(expert_all[:, bass.ds(i, 1), k * NT:k * NT + NT].rearrange("p a n -> p (a n)"),
                                  top_f[:, :, k]).then_inc(kept, 1)
                v.tensor_copy(gates_all[:, bass.ds(i, 1), :].rearrange("p a n -> p (a n)"),
                              gts[:].rearrange("p k t -> p (k t)")).then_inc(kept, 1)

            dve.wait_ge(weights_in, 16 * len(WEIGHTS))
            v.tensor_copy(tri[:], cst[:, C_TRI:C_TRI + P]).then_inc(const_made, 1)
            v.memset(ones[:], 1.0).then_inc(const_made, 1)
            v.tensor_copy(base[:], cst[:, C_BASE:C_BASE + E]).then_inc(const_made, 1)
            v.memset(kT[:], 0.0).then_inc(const_made, 1)
            v.memset(zeros[:], 0.0).then_inc(const_made, 1)
            dve.wait_ge(const_made, 5)
            norm_stats(0)
            norm_apply(0)
            gate_copy(0)
            gate_min(0)
            gate_sums(0)
            keys(0)
            queries(0)
            states(0)
            with dve.Fori(0, S - 1) as i:
                chunks(i, True)
                keys(i + 1)
                queries(i + 1)
                merged(i, NT - 1)
                states(i + 1)
                route(i)
            chunks(S - 1, False)
            merged(S - 1, NT - 1)
            route(S - 1)

            steps = [0]

            def link(ins):
                steps[0] += 1
                ins.then_inc(dve_step, 1)
                dve.wait_ge(dve_step, steps[0])

            dve.wait_ge(base_ready, FIRST + S)
            dve.wait_ge(kept, 4 * S)
            link(v.tensor_copy(end_i[:], base[:]))
            link(v.tensor_tensor(cnt[:], base[:], cst[:, C_BASE:C_BASE + E], ALU.subtract))
            link(v.tensor_scalar(cnt[:], cnt[:], float(ROWS - 1), None, ALU.add))
            link(v.tensor_copy(cnt_i[:], cnt[:]))
            link(v.tensor_scalar(til_i[:], cnt_i[:], ROWS.bit_length() - 1, None, ALU.arith_shift_right))
            link(v.tensor_copy(til[:], til_i[:]))
            link(v.tensor_scalar(til[:], til[:], 1.0, None, ALU.max))
            link(v.tensor_tensor_scan(cum[:], ones_row, til[:], 0.0, ALU.mult, ALU.add))
            link(v.tensor_copy(cum_i[:], cum[:]))
            n1 = TILES + 1
            link(v.tensor_tensor(tge[:], wide(tnum.unsqueeze(2), 1, n1, E),
                                 wide(cum[0:1, :].unsqueeze(1), 1, n1, E), ALU.is_ge))
            link(v.tensor_tensor(tmul[:], tge[:], wide(til[0:1, :].unsqueeze(1), 1, n1, E), ALU.mult))
            link(v.tensor_reduce(te[:], tge[:], AX, ALU.add))
            link(v.tensor_reduce(tprev[:], tmul[:], AX, ALU.add))
            link(v.tensor_tensor(trow[:], tnum, tprev[:], ALU.subtract))
            link(v.tensor_scalar(trow[:], trow[:], float(ROWS), None, ALU.mult))
            link(v.scalar_tensor_tensor(out=trow[:], in0=te[:], scalar=float(CAP), in1=trow[:],
                                        op0=ALU.mult, op1=ALU.add))
            link(v.tensor_scalar(trow[:], trow[:], float(E * CAP), None, ALU.min))
            v.tensor_copy(trow_i[:], trow[:]).then_inc(counts_ready, 1)
            link(v.tensor_tensor(shift[:], cum[:], til[:], ALU.subtract))
            link(v.scalar_tensor_tensor(out=shift[:], in0=shift[:], scalar=float(ROWS),
                                        in1=cst[:, C_BASE:C_BASE + E], op0=ALU.mult, op1=ALU.subtract))
            n2 = S * 2 * NT
            link(v.tensor_tensor(chosen, wide(iota8.unsqueeze(1), P, n2, E),
                                 wide(expert_all[:].rearrange("p s n -> p (s n)").unsqueeze(2), P, n2, E),
                                 ALU.is_equal))
            link(v.tensor_tensor(chosen, chosen, wide(shift[:].unsqueeze(1), P, n2, E), ALU.mult))
            link(v.tensor_reduce(result_f[:], chosen, AX, ALU.add))
            link(v.tensor_tensor(result_f[:], result_f[:], rows_all[:].rearrange("p s n -> p (s n)"), ALU.add))
            link(v.tensor_copy(result_i[:].rearrange("p s n -> p (s n)"), result_f[:]))
            dve.wait_ge(counts_ready, 1)

            total = dve.value_load(cum_i[0:1, E - 1:E], min_val=E, max_val=TILES)
            bank = [pA[0][:].rearrange("p a c -> p (a c)"), pA[1][:].rearrange("p a c -> p (a c)"),
                    pJ[0][:], pJ[1][:]]
            with dve.Fori(0, total) as t:
                for f in range(FB):
                    dve.wait_ge(silu_ready, t * FB + f + 1)
                    if f == 0:
                        dve.wait_ge(y_psum, FIRST + t)
                    v.tensor_tensor(hT[:, f, :], bank[f][:, ROWS:2 * ROWS], sil[:, f, :], ALU.mult)\
                        .then_inc(h_ready, 1)

            with dve.Fori(0, S) as i:
                v.tensor_copy(cidx[:], result_i[:, bass.ds(i, 1), :].rearrange("p a n -> p (a n)"))\
                    .then_inc(c_idx, 1)
                v.tensor_copy(cgate[:].rearrange("p k t -> p (k t)"),
                              gates_all[:, bass.ds(i, 1), :].rearrange("p a n -> p (a n)")).then_inc(c_idx, 1)
                dve.wait_ge(c_idx, i * 2 + 2)
                dve.wait_ge(c_gath, i * (16 * 2 * NT) + 16 * 2 * NT)
                for k in range(2):
                    v.tensor_tensor(cy[:, k, :, :], cy[:, k, :, :], wide(cgate[:, k, :].unsqueeze(2), P, NT, HID),
                                    ALU.mult).then_inc(c_mul, 1)
                dve.wait_ge(c_mul, i * 2 + 2)
                v.tensor_tensor(cf[:], cy[:, 0, :, :], cy[:, 1, :, :], ALU.add).then_inc(c_sum, 1)
                dve.wait_ge(c_sum, FIRST + i + 1)
                for t in range(NT):
                    v.bn_stats(st[:, 0, t, :], cf[:, t, :]).then_inc(c_stat, 1)
                dve.wait_ge(c_stat, i * 2 * NT + NT)
                settle(dve)
                for t in range(NT):
                    v.bn_aggr(mv[:, 0, t, :], st[:, 0, t, :]).then_inc(c_stat, 1)
                dve.wait_ge(c_rstd, i + 1)
                for t in range(NT):
                    v.tensor_scalar(cn[:, t, :], cf[:, t, :], mv[:, 0, t, 0:1], rstd[:, 0, t:t + 1],
                                    ALU.subtract, ALU.mult).then_inc(c_norm, 1)
                dve.wait_ge(c_norm, i * NT + NT)
                dve.wait_ge(c_x1, i * 16 + 16)
                dve.wait_ge(c_out, FIRST + i * 16)
                v.tensor_tensor(co[:], cn[:], cx[:], ALU.add).then_inc(c_res, 1)

        @block.gpsimd
        def _(pool):
            g = nc.gpsimd

            def mids(j):
                pool.wait_ge(step_ready, j + 1)
                settle(pool)
                for c in range(NC - 1):
                    pool.wait_ge(raw_ready, j * (NC - 1) + c + 1)
                    settle(pool)
                    g.tensor_tensor(S_mid[:, c + 1, :, :], S_raw[:, c % 2, :, :],
                                    wide(step[:, :, c:c + 1], P, PAIRS, P), ALU.mult).then_inc(mid_ready, 1)

            def residual(i, t):
                pool.wait_ge(an_ready, i * NT + t + 1)
                settle(pool)
                pool.wait_ge(xr_in, i * 16 + 16)
                settle(pool)
                if t == 0:
                    pool.wait_ge(x1_out, FIRST + i * 16)
                    settle(pool)
                    pool.wait_ge(x1n_ready, FIRST + i * NT)
                    settle(pool)
                g.tensor_tensor(x1[:, t, :], an[:, t, :], xr[:, t, :], ALU.add).then_inc(x1_ready, 1)

            def scatter(i, k, t):
                pool.wait_ge(rowi_ready, i + 1)
                settle(pool)
                g.indirect_dma_start(out=xs_dram, out_offset=bass.IndirectOffsetOnAxis(ap=rowi[:, k, t:t + 1], axis=0),
                                     in_=x1n[:, t, :], in_offset=None).then_inc(scattered, 16)

            g.memset(vJ[:], 0.0).then_inc(vJ_zero, 1)
            mids(0)
            with pool.Fori(0, S - 1) as i:
                for t in range(NT - 1):
                    residual(i, t)
                residual(i, NT - 1)
                mids(i + 1)
                for t in range(NT):
                    for k in range(2):
                        scatter(i, k, t)
                pool.wait_ge(scattered, (i + 1) * (16 * 2 * NT))
                pool.sem_inc(rows_free, 1)
            for t in range(NT):
                residual(S - 1, t)
            for t in range(NT):
                for k in range(2):
                    scatter(S - 1, k, t)

            pool.wait_ge(counts_ready, 1)
            total = pool.value_load(cum_i[0:1, E - 1:E], min_val=E, max_val=TILES)
            pool.wait_ge(y_out, FIRST + total * 16)
            settle(pool)
            with pool.Fori(0, S) as i:
                pool.wait_ge(c_idx, i * 2 + 2)
                settle(pool)
                pool.wait_ge(c_sum, FIRST + i)
                settle(pool)
                for k in range(2):
                    for t in range(NT):
                        g.indirect_dma_start(
                            out=cy[:, k, t, :], out_offset=None, in_=ys_dram,
                            in_offset=bass.IndirectOffsetOnAxis(ap=cidx[:, k * NT + t:k * NT + t + 1], axis=0))\
                            .then_inc(c_gath, 16)


def kernel(**inputs):
    import concourse.bacc as _bacc
    from concourse.bass_utils import run_bass_kernel_spmd as _run

    g = {n.removeprefix("L0_"): np.asarray(a) for n, a in inputs.items()}
    x = np.ascontiguousarray(g["attn_hidden_states"])
    tiles = 2 * x.shape[0] * x.shape[1] // ROWS + E
    cap = x.shape[0] * x.shape[1] + ROWS
    c = np.zeros((P, C_TNUM + tiles + 1), np.float32)
    c[:, C_IDENT:C_IDENT + P] = np.eye(P)
    c[:, C_MASK:C_MASK + C] = np.tile(np.triu(np.ones((C, C))), (2, 1))
    c[:, C_TRI:C_TRI + P] = np.triu(np.ones((P, P)), 1)
    c[:, C_IOTA:C_IOTA + E] = np.arange(E)
    c[:, C_SCAN:C_SCAN + 1024] = np.arange(1024) % C != 0
    c[:, C_EPS_HEAD] = D * NORM_EPS
    c[:, C_EPS_LN] = LN_EPS
    c[:, C_BASE:C_BASE + E] = np.arange(E) * cap
    c[:, C_ONES:C_ONES + E] = 1
    c[:, C_TNUM:] = np.arange(tiles + 1)
    arrays = {
        "x": x,
        "wq": g["attn_Wq"].reshape(HID, PAIRS, 2, R, D).transpose(0, 1, 3, 2, 4).reshape(HID, PAIRS, R, P),
        "wk": g["attn_Wk"].reshape(HID, PAIRS, P),
        "wv": g["attn_Wv"],
        "wo": g["attn_Wo"].reshape(PAIRS, 2, R, D, HID).transpose(1, 3, 0, 2, 4).reshape(P, PAIRS * R, HID),
        "wg1": g["attn_Wg1"],
        "wg2": g["attn_Wg2"].reshape(LOW, PAIRS, P),
        "bg2": g["attn_bg2"].reshape(PAIRS, P).T,
        "gnorm": np.concatenate([g["attn_g_norm_weight"]] * 2).reshape(P, 1),
        "rw": g["ffn_router_w"].T,
        "rb": g["ffn_router_b"].reshape(1, E),
        "wgate": g["ffn_gate_w"].transpose(2, 0, 1),
        "wup": g["ffn_up_w"].transpose(2, 0, 1),
        "wdown": g["ffn_down_w"].reshape(E, HID, FB, P).transpose(3, 0, 2, 1),
        "consts": c,
    }
    arrays = {n: np.ascontiguousarray(a) for n, a in arrays.items()}
    nc = _bacc.Bacc("TRN2", target_bir_lowering=False, num_devices=1)
    args = [nc.dram_tensor(n, a.shape, F32, kind="ExternalInput").ap() for n, a in arrays.items()]
    out = nc.dram_tensor("out", x.shape, F32, kind="ExternalOutput").ap()
    build(nc, *args, out)
    r = _run(nc, [arrays], core_ids=[0])
    return r.results[0]["out"]
```

```python
from contextlib import ExitStack

import numpy as np

import concourse.bass as bass
from concourse import mybir

P = 128
F32 = mybir.dt.float32
U32 = mybir.dt.uint32
I32 = mybir.dt.int32
BF16 = mybir.dt.bfloat16
ALU = mybir.AluOpType
ACT = mybir.ActivationFunctionType
LOG_EXP = "natural_log_exp_and_others"
AX = mybir.AxisListType.X

D = 64
C = 64
HID = 128
LOW = 16
PAIRS = 2
R = 4
E = 8
FF = 512
FB = FF // P
ROWS = 256
XW = HID + 2
NORM_EPS = 1e-6
LN_EPS = 1e-5
GATE_NORMALIZER = 16.0

C_IDENT, C_MASK, C_TRI, C_IOTA, C_SCAN = 0, 128, 192, 320, 328
C_EPS_HEAD, C_EPS_LN = C_SCAN + 1024, C_SCAN + 1025
C_BASE = C_SCAN + 1026
C_ONES = C_BASE + 8
C_GOAL = C_ONES + 8
C_PAD = C_GOAL + 8
C_TNUM = C_PAD + 2



def build(nc, x, wq, wk, wv, wo, wg1, wg2, bg2, gnorm, rw, rb, wgate, wup, wdown, consts, out):
    S, L, _ = x.shape
    NC = L // C
    NT = L // P
    T = S * L
    CAP = T + ROWS
    TILES = 2 * T // ROWS + E

    ctx = ExitStack()
    with ctx:
        def sb(name, shape, dt=F32):
            return ctx.enter_context(nc.sbuf_tensor(name, shape, dt))

        def ps(name, shape):
            return ctx.enter_context(nc.psum_tensor(name, shape, F32))

        def sem(name):
            return ctx.enter_context(nc.semaphore(name))

        xs_dram = nc.dram_tensor("expert_rows", (E * CAP + ROWS, XW), F32).ap()
        ys_dram = nc.dram_tensor("expert_out", (2 * T + ROWS, HID), F32).ap()
        x1_dram = nc.dram_tensor("after_attention", (T, HID), F32).ap()

        cst = sb("cst", [P, C_TNUM + TILES + 1])
        wq_sb = sb("wq_sb", [P, PAIRS, R, P])
        wk_sb = sb("wk_sb", [P, PAIRS, P])
        wv_sb = sb("wv_sb", [P, 2 * PAIRS * D])
        wo_sb = sb("wo_sb", [P, PAIRS * R, HID])
        wg1_sb = sb("wg1_sb", [P, LOW])
        wg2_sb = sb("wg2_sb", [LOW, PAIRS, P])
        bg2_sb = sb("bg2_sb", [P, PAIRS])
        nbg2_sb = sb("nbg2_sb", [P, PAIRS])
        gn_sb = sb("gn_sb", [P, 1])
        rw_sb = sb("rw_sb", [P, E])
        rb_sb = sb("rb_sb", [P, E])
        wgate_sb = sb("wgate_sb", [P, E, FF])
        wup_sb = sb("wup_sb", [P, E, FF])
        wdown_sb = sb("wdown_sb", [P, E, FB, HID])
        ident = cst[:, C_IDENT:C_IDENT + P]
        causal = cst[:, C_MASK:C_MASK + C]
        iota8 = cst[:, C_IOTA:C_IOTA + E]
        tnum = cst[0:1, C_TNUM:C_TNUM + TILES + 1]
        ones_row = cst[:, C_ONES:C_ONES + E]
        in_chunk = cst[:, C_SCAN:C_SCAN + 1024]
        tri = sb("tri", [P, P], BF16)
        ones = sb("ones", [P, P], BF16)
        zeros = sb("zeros", [P, 2, XW])

        xa = sb("xa", [P, NT, HID])
        xr = sb("xr", [P, NT, HID])
        xn = sb("xn", [P, NT, HID])
        xnT = sb("xnT", [P, NC, 2, C])
        h1 = sb("h1", [LOW, L])
        absz = sb("absz", [P, PAIRS, L])
        relz = sb("relz", [P, PAIRS, L])
        run = sb("run", [P, PAIRS, L])
        rel = sb("rel", [P, PAIRS, L])
        grow = sb("grow", [P, PAIRS, L])
        shrink = sb("shrink", [P, PAIRS, L])
        step_log = sb("step_log", [P, PAIRS, NC])
        step = sb("step", [P, PAIRS, NC])
        qT = sb("qT", [P, PAIRS, NC, R, C])
        kT = sb("kT", [P, PAIRS, NC, P])
        kJ = sb("kJ", [P, NC, PAIRS, P])
        vJ = sb("vJ", [P, NC, PAIRS, P])
        S_raw = sb("S_raw", [P, 2, PAIRS, P])
        S_mid = sb("S_mid", [P, NC, PAIRS, P])
        aT = sb("aT", [P, 2, PAIRS, R * C])
        sq = sb("sq", [P, 2, 512])
        ss = sb("ss", [P, 2, 8])
        lnss = sb("lnss", [P, 2, 8])
        rs = sb("rs", [P, 2, 8])
        on = sb("on", [P, 2, 4, P])
        oT = sb("oT", [P, 2, PAIRS * R, 2, C])
        st = sb("st", [P, 3, NT, 6])
        mv = sb("mv", [P, 3, NT, 2])
        lnv = sb("lnv", [P, 3, NT])
        rstd = sb("rstd", [P, 3, NT])
        an = sb("an", [P, NT, HID])
        x1 = sb("x1", [P, NT, HID])
        x1n = sb("x1n", [P, 2, NT, XW])
        x1nT = sb("x1nT", [P, NT, P])

        logit = sb("logit", [P, NT, E])
        top = sb("top", [P, NT, 8])
        top_i = sb("top_i", [P, NT, 8], U32)
        top_f = sb("top_f", [P, NT, 8])
        pick = sb("pick", [P, 2, NT, E])
        both = sb("both", [P, NT, E], BF16)
        place = sb("place", [P, NT, E])
        base = sb("base", [P, E])
        placed = sb("placed", [P, 2, NT, E])
        rowf = sb("rowf", [P, 2, NT])
        rowi = sb("rowi", [P, 2, NT], U32)
        diff = sb("diff", [P, NT])
        ediff = sb("ediff", [P, NT])
        den = sb("den", [P, NT])
        gts = sb("gts", [P, 2, NT])
        goal = sb("goal", [P, 2, NT])

        cnt = sb("cnt", [P, E])
        cnt_i = sb("cnt_i", [P, E], I32)
        til_i = sb("til_i", [P, E], I32)
        til = sb("til", [P, E])
        cum = sb("cum", [P, E])
        cum_i = sb("cum_i", [P, E], U32)
        end_i = sb("end_i", [P, E], U32)
        tge = sb("tge", [1, TILES + 1, E])
        tmul = sb("tmul", [1, TILES + 1, E])
        te = sb("te", [1, TILES + 1])
        tprev = sb("tprev", [1, TILES + 1])
        trow = sb("trow", [1, TILES + 1])
        trow_i = sb("trow_i", [1, TILES + 1], U32)

        xt = sb("xt", [P, 2, XW])
        tail_next = sb("tail_next", [P, 2, 2])
        tail = sb("tail", [P, 2, 2])
        xtT = sb("xtT", [P, ROWS])
        y = sb("y", [P, 2, HID])
        sil = kJ[:].rearrange("p n a j -> p (n a j)")[:, 0:FB * ROWS].rearrange("p (f n) -> p f n", f=FB)
        hT = vJ[:].rearrange("p n a j -> p (n a j)")[:, 0:FB * ROWS].rearrange("p (f n) -> p f n", f=FB)
        cbuf = qT[:].rearrange("p a n r c -> p (a n r c)").rearrange("p (b k t h) -> p b k t h", b=2, k=4, t=NT)
        cn = S_mid[:].rearrange("p n a j -> p (n a j)")[:, 0:2 * NT * HID].rearrange("p (b t h) -> p b t h", b=2, t=NT)

        pA = [ps(f"pA{n}", [P, PAIRS, R * C]) for n in range(2)]
        pO = [ps(f"pO{n}", [P, 4, P]) for n in range(2)]
        pJ = [ps(f"pJ{n}", [P, 512]) for n in range(2)]
        pT = ps("pT", [P, 512])
        pW = ps("pW", [P, 512])

        four = [pA[0][:].rearrange("p a c -> p (a c)"), pA[1][:].rearrange("p a c -> p (a c)"), pJ[0][:], pJ[1][:]]
        key_bank = [pO[0][:].rearrange("p k v -> p (k v)"), pO[1][:].rearrange("p k v -> p (k v)"), pT[:]]
        key_bank.append(key_bank[0])

        def query_turn(n):
            b = n if n < 2 else 1 + n // 2 if n % 2 else None
            return b if b is not None and b < PAIRS * R else None

        def state_turn(n):
            c = n // 2 - 1 if n % 2 == 0 and n >= 2 else None
            return c

        block = ctx.enter_context(nc.Block())
        tail_ready = sem("tail_ready")
        goal_ready = sem("goal_ready")
        copied = sem("copied")
        tail_next_ready = sem("tail_next_ready")
        tail_kept = sem("tail_kept")
        y_free = sem("y_free")
        c_in = [sem(f"c_in{b}") for b in range(2)]
        c_out_before = sem("c_out_before")
        settled = sem("settled")
        rows_free = sem("rows_free")
        vJ_zero = sem("vJ_zero")
        weights_in = sem("weights_in")
        const_made = sem("const_made")
        xa_in = sem("xa_in")
        xr_in = sem("xr_in")
        x1_out = sem("x1_out")
        xn_stat = sem("xn_stat")
        xn_rstd = sem("xn_rstd")
        xn_lnv = sem("xn_lnv")
        xn_ready = sem("xn_ready")
        xnT_psum = sem("xnT_psum")
        xnT_ready = sem("xnT_ready")
        h1_psum = sem("h1_psum")
        h1_ready = sem("h1_ready")
        z_psum = sem("z_psum")
        absz_ready = sem("absz_ready")
        relz_ready = sem("relz_ready")
        ez_ready = sem("ez_ready")
        lz_ready = sem("lz_ready")
        gate_ready = sem("gate_ready")
        run_ready = sem("run_ready")
        rel_ready = sem("rel_ready")
        steplog_ready = sem("steplog_ready")
        decay_ready = sem("decay_ready")
        step_ready = sem("step_ready")
        k_psum = sem("k_psum")
        k_ready = sem("k_ready")
        v_psum = sem("v_psum")
        v_ready = sem("v_ready")
        q_psum = sem("q_psum")
        q_ready = sem("q_ready")
        kJ_psum = sem("kJ_psum")
        kJ_ready = sem("kJ_ready")
        upd_psum = sem("upd_psum")
        raw_ready = sem("raw_ready")
        mid_ready = sem("mid_ready")
        a_psum = sem("a_psum")
        a_ready = sem("a_ready")
        o_psum = sem("o_psum")
        sq_ready = sem("sq_ready")
        ss_ready = sem("ss_ready")
        lnss_ready = sem("lnss_ready")
        rs_ready = sem("rs_ready")
        on_ready = sem("on_ready")
        ot_psum = sem("ot_psum")
        ot_ready = sem("ot_ready")
        w_psum = sem("w_psum")
        w_stat = sem("w_stat")
        w_lnv = sem("w_lnv")
        w_rstd = sem("w_rstd")
        an_ready = sem("an_ready")
        x1_ready = sem("x1_ready")
        r_stat = sem("r_stat")
        r_aggr = sem("r_aggr")
        r_lnv = sem("r_lnv")
        r_rstd = sem("r_rstd")
        x1n_ready = sem("x1n_ready")
        x1nT_psum = sem("x1nT_psum")
        x1nT_ready = sem("x1nT_ready")
        logit_psum = sem("logit_psum")
        logit_ready = sem("logit_ready")
        top_ready = sem("top_ready")
        topi_ready = sem("topi_ready")
        topf_ready = sem("topf_ready")
        pick_ready = sem("pick_ready")
        both_ready = sem("both_ready")
        rank_psum = sem("rank_psum")
        place_ready = sem("place_ready")
        base_ready = sem("base_ready")
        placed_ready = sem("placed_ready")
        rowf_ready = sem("rowf_ready")
        rowi_ready = sem("rowi_ready")
        diff_ready = sem("diff_ready")
        ediff_ready = sem("ediff_ready")
        den_ready = sem("den_ready")
        g1_ready = sem("g1_ready")
        g2_ready = sem("g2_ready")
        kept = sem("kept")
        scattered = sem("scattered")
        dve_step = sem("dve_step")
        counts_ready = sem("counts_ready")
        tail_in = sem("tail_in")
        pad_out = sem("pad_out")
        xt_in = sem("xt_in")
        xt_psum = sem("xt_psum")
        xt_ready = sem("xt_ready")
        up_psum = sem("up_psum")
        silu_ready = sem("silu_ready")
        h_ready = sem("h_ready")
        y_psum = sem("y_psum")
        y_ready = sem("y_ready")
        y_out = sem("y_out")
        c_sum = sem("c_sum")
        c_stat = sem("c_stat")
        c_lnv = sem("c_lnv")
        c_rstd = sem("c_rstd")
        c_norm = sem("c_norm")
        c_res = sem("c_res")
        c_out = sem("c_out")

        FIRST = 1

        def at_start(j):
            return isinstance(j, int) and j == 0

        def settle(eng):
            eng.sem_inc(settled, 1)

        xv = x.rearrange("s (t p) h -> s p t h", p=P)
        x1v = x1_dram.rearrange("(s t p) h -> s p t h", p=P, t=NT)
        ov = out.rearrange("s (t p) h -> s p t h", p=P)

        def seq(v, i):
            return v[bass.ds(i, 1)].rearrange("a p t h -> p (a t) h")

        def wide(ap, *shape):
            return ap.to_broadcast(list(shape))

        WEIGHTS = [(wq_sb, wq), (wk_sb, wk), (wv_sb, wv), (wo_sb, wo), (wg1_sb, wg1), (wg2_sb, wg2),
                   (bg2_sb, bg2), (gn_sb, gnorm), (rw_sb, rw), (rb_sb, rb.to_broadcast([P, E])), (cst, consts)]
        BIG = [(wgate_sb, wgate), (wup_sb, wup), (wdown_sb, wdown)]

        @block.sync
        def _(sp):
            for credited in (x1_ready, x1nT_ready, base_ready, x1_out, x1n_ready, rows_free, h_ready,
                             y_ready, y_free, y_psum, tail_kept, c_out_before):
                sp.sem_inc(credited, FIRST)
            sp.dma_start(xa[:], seq(xv, 0)).then_inc(xa_in, 16)
            for dst, src in WEIGHTS:
                sp.dma_start(dst[:], src).then_inc(weights_in, 16)
            for dst, src in BIG:
                sp.dma_start(dst[:], src).then_inc(tail_in, 16)

            def sequence(i, more):
                if more:
                    sp.wait_ge(xn_ready, (i + 1) * NT)
                    settle(sp)
                    sp.dma_start(xa[:], seq(xv, i + 1)).then_inc(xa_in, 16)
                sp.wait_ge(x1_ready, FIRST + i * NT)
                settle(sp)
                sp.dma_start(xr[:], seq(xv, i)).then_inc(xr_in, 16)
                sp.wait_ge(x1_ready, FIRST + (i + 1) * NT)
                settle(sp)
                sp.dma_start(seq(x1v, i), x1[:]).then_inc(x1_out, 16)

            sequence(0, True)
            with sp.Fori(1, S - 1) as i:
                sequence(i, True)
            sequence(S - 1, False)

            sp.wait_ge(counts_ready, 1)
            for e in range(E):
                first = sp.value_load(end_i[0:1, e:e + 1], min_val=e * CAP, max_val=e * CAP + T)
                sp.dma_start(xs_dram[bass.ds(first, ROWS)].rearrange("(t p) h -> p t h", p=P),
                             zeros[:]).then_inc(pad_out, 16)
            sp.dma_start(xs_dram[E * CAP:E * CAP + ROWS].rearrange("(t p) h -> p t h", p=P),
                         zeros[:]).then_inc(pad_out, 16)
            sp.wait_ge(pad_out, 16 * (E + 1))
            sp.wait_ge(scattered, 16 * 2 * NT * S)

            def load_tile(t):
                first = sp.value_load(trow_i[0:1, bass.ds(t, 1)], min_val=0, max_val=E * CAP)
                sp.dma_start(xt[:], xs_dram[bass.ds(first, ROWS)].rearrange("(t p) h -> p t h", p=P))\
                  .then_inc(xt_in, 16)
                return first

            load_tile(0)
            total = sp.value_load(cum_i[0:1, E - 1:E], min_val=E, max_val=TILES)
            with sp.Fori(0, total) as t:
                sp.wait_ge(xt_psum, t + 1)
                settle(sp)
                sp.wait_ge(tail_next_ready, t + 1)
                settle(sp)
                load_tile(t + 1)
            sp.wait_ge(xt_in, total * 16 + 16)
            settle(sp)

            sp.wait_ge(y_out, total * 32)
            settle(sp)

            yv = ys_dram[0:2 * T].rearrange("(k s t p) h -> k s p t h", p=P, t=NT, s=S)

            def loads(i, b):
                for k in range(2):
                    sp.dma_start(cbuf[:, b, k, :, :], seq(yv[k], i)).then_inc(c_in[b], 16)
                sp.dma_start(cbuf[:, b, 2, :, :], seq(x1v, i)).then_inc(c_in[b], 16)

            for b in range(2):
                loads(b, b)
            with sp.Fori(0, S // 2 - 1) as n:
                for b in range(2):
                    sp.wait_ge(c_res, n * 2 + b + 1)
                    settle(sp)
                    loads(n * 2 + 2 + b, b)
            sp.wait_ge(c_out, S * 16)

        @block.tensor
        def _(pe):
            mm, tr = nc.tensor.matmul, nc.tensor.transpose

            def norm_transposes(j):
                pe.wait_ge(xn_ready, j * NT + NT)
                if not at_start(j):
                    pe.wait_ge(x1nT_ready, FIRST + j - 1)
                for t in range(NT):
                    last = tr(pW[:, t * P:(t + 1) * P], xn[:, t, :], ident)
                last.then_inc(xnT_psum, 1)

            def gate_low(j):
                pe.wait_ge(xnT_ready, j * 2 + 2)
                mm(pJ[0][0:LOW, :], wg1_sb[:], xnT[:, :, 0, :], start=True, stop=True).then_inc(h1_psum, 1)

            def gate_high(j, routed=False):
                pe.wait_ge(h1_ready, j + 1)
                for p in range(PAIRS):
                    if routed and p == 1:
                        pe.wait_ge(base_ready, FIRST + j - 1)
                    mm(pJ[p][:], wg2_sb[:, p, :], h1[:], start=True, stop=True).then_inc(z_psum, 1)

            def project_keys(j):
                pe.wait_ge(relz_ready, j * 2 + 2)
                for p in range(PAIRS):
                    mm(pJ[p][:], wk_sb[:, p, :], xnT[:, :, 0, :], start=True, stop=True).then_inc(k_psum, 1)

            def project_values(j):
                for g in range(NC // 2):
                    if g < 2:
                        if g == 0 and not at_start(j):
                            pe.wait_ge(a_ready, j * NC)
                    else:
                        pe.wait_ge(k_ready, j * 4 + 2 * g - 2)
                    for c in (2 * g, 2 * g + 1):
                        last = mm(four[g][:, (c % 2) * 256:(c % 2) * 256 + 256],
                                  xnT[:, c, :, :].rearrange("p a c -> p (a c)"), wv_sb[:], start=True, stop=True)
                    last.then_inc(v_psum, 1)

            def key_transposes(j):
                pe.wait_ge(k_ready, j * 4 + 4)
                for g in range(NC // 2):
                    if g == 3:
                        pe.wait_ge(kJ_ready, j * 4 + 1)
                    elif not at_start(j):
                        pe.wait_ge(*((on_ready, j * NC), (on_ready, j * NC), (ot_ready, j * NC))[g])
                    for c in range(2 * g, min(2 * g + 2, NC - 1)):
                        for p in range(PAIRS):
                            last = tr(key_bank[g][:, ((c % 2) * 2 + p) * P:((c % 2) * 2 + p + 1) * P],
                                      kT[:, p, c, :], ident)
                    last.then_inc(kJ_psum, 1)

            def project_queries_and_states(j):
                for n in range(2 * PAIRS * R):
                    b = query_turn(n)
                    if b is not None:
                        if b < 4:
                            pe.wait_ge(v_ready, j * NC + 2 * b + 2)
                        else:
                            pe.wait_ge(q_ready, j * 8 + b - 3)
                        mm(four[b % 4][:], wq_sb[:, b // R, b % R, :], xnT[:, :, 0, :],
                           start=True, stop=True).then_inc(q_psum, 1)
                    c = state_turn(n)
                    if c is not None:
                        pe.wait_ge(kJ_ready, j * 4 + (4 if c < 2 else c // 2 + 1))
                        if c >= 2:
                            pe.wait_ge(raw_ready, j * (NC - 1) + c - 1)
                        for p in range(PAIRS):
                            last = mm(pO[c % 2][:, p, :], kJ[:, c, p, :], vJ[:, c, p, :], start=True, stop=True)
                        last.then_inc(upd_psum, 1)

            def scores(i, c):
                pe.wait_ge(q_ready, i * 8 + 8)
                if c >= 2:
                    pe.wait_ge(a_ready, i * NC + c - 1)
                for p in range(PAIRS):
                    last = mm(pA[c % 2][:, p, :], kT[:, p, c, :],
                              qT[:, p, c, :, :].rearrange("p r c -> p (r c)"), start=True, stop=True)
                last.then_inc(a_psum, 1)

            def outputs(i, c):
                pe.wait_ge(a_ready, i * NC + c + 1)
                if c >= 2:
                    pe.wait_ge(on_ready, i * NC + c - 1)
                else:
                    pe.wait_ge(raw_ready, i * (NC - 1) + NC - 1)
                if c > 0:
                    pe.wait_ge(mid_ready, i * (NC - 1) + c)
                for p in range(PAIRS):
                    for h in range(2):
                        o = pO[c % 2][:, 2 * p + h, :]
                        last = mm(o, aT[:, c % 2, p, h * P:(h + 1) * P], vJ[:, c, p, :], start=True, stop=(c == 0))
                        if c > 0:
                            last = mm(o, qT[:, p, c, 2 * h:2 * h + 2, :].rearrange("p r c -> p (r c)"),
                                      S_mid[:, c, p, :], start=False, stop=True)
                last.then_inc(o_psum, 1)

            def out_transposes(i, c):
                pe.wait_ge(on_ready, i * NC + c + 1)
                if c > 0:
                    pe.wait_ge(ot_ready, i * NC + c)
                for k in range(4):
                    last = tr(pT[:, k * P:(k + 1) * P], on[:, c % 2, k, :], ident)
                last.then_inc(ot_psum, 1)

            def merge_heads(i, t, more):
                pe.wait_ge(ot_ready, i * NC + 2 * t + 2)
                if t > 0:
                    pe.wait_ge(an_ready, i * NT + t)
                elif more:
                    pe.wait_ge(xnT_ready, i * 2 + 4)
                else:
                    pe.wait_ge(x1nT_ready, FIRST + i)
                for b in range(PAIRS * R):
                    last = mm(pW[:, 0:HID], oT[:, t % 2, b, :, :].rearrange("p a c -> p (a c)"), wo_sb[:, b, :],
                              start=(b == 0), stop=(b == PAIRS * R - 1))
                last.then_inc(w_psum, 1)

            def chunks(i, more, routed):
                scores(i, 0)
                for c in range(NC):
                    if c + 1 < NC:
                        scores(i, c + 1)
                    if routed and c == 2:
                        router_transposes(i - 1)
                    if routed and c == 4:
                        ranks(i - 1)
                    if more and c == 5:
                        gate_high(i + 1, routed)
                    outputs(i, c)
                    if c > 0:
                        out_transposes(i, c - 1)
                    if routed and c == 2:
                        logits(i - 1)
                    if more and c == 2:
                        norm_transposes(i + 1)
                    if more and c == 3:
                        gate_low(i + 1)
                    if c in (3, 5, 7):
                        merge_heads(i, (c - 3) // 2, more)

            def router_transposes(i):
                pe.wait_ge(x1n_ready, FIRST + i * NT + NT)
                for t in range(NT):
                    last = tr(pW[:, t * P:(t + 1) * P], x1n[:, 0, t, 0:HID], ident)
                last.then_inc(x1nT_psum, 1)

            def logits(i):
                pe.wait_ge(x1nT_ready, FIRST + i + 1)
                for t in range(NT):
                    last = mm(pJ[1][:, t * E:(t + 1) * E], x1nT[:, t, :], rw_sb[:], start=True, stop=True)
                last.then_inc(logit_psum, 1)

            def ranks(i):
                pe.wait_ge(both_ready, i + 1)
                for t in range(NT + 1):
                    o = pJ[1][:, t * E:(t + 1) * E]
                    for u in range(min(t, NT)):
                        last = mm(o, ones[:], both[:, u, :], start=(u == 0), stop=(t == NT and u == NT - 1))
                    if t < NT:
                        last = mm(o, tri[:], both[:, t, :], start=(t == 0), stop=True)
                last.then_inc(rank_psum, 1)

            pe.wait_ge(weights_in, 16 * len(WEIGHTS))
            pe.wait_ge(const_made, 8)
            norm_transposes(0)
            gate_low(0)
            gate_high(0)
            project_keys(0)
            project_values(0)
            key_transposes(0)
            project_queries_and_states(0)

            def turn(i, routed):
                chunks(i, True, routed)
                project_keys(i + 1)
                out_transposes(i, NC - 1)
                project_values(i + 1)
                key_transposes(i + 1)
                merge_heads(i, NT - 1, True)
                project_queries_and_states(i + 1)

            turn(0, False)
            with pe.Fori(1, S - 1) as i:
                turn(i, True)
            chunks(S - 1, False, True)
            out_transposes(S - 1, NC - 1)
            merge_heads(S - 1, NT - 1, False)
            router_transposes(S - 1)
            pe.wait_ge(base_ready, FIRST + S - 1)
            logits(S - 1)
            ranks(S - 1)

            def rows_transposed(t):
                pe.wait_ge(xt_in, t * 16 + 16)
                for k in range(2):
                    last = tr(pT[:, k * P:(k + 1) * P], xt[:, k, 0:HID], ident)
                last.then_inc(xt_psum, 1)

            pe.wait_ge(tail_in, 16 * len(BIG))
            pe.wait_ge(counts_ready, 1)
            bank = [pA[0][:].rearrange("p a c -> p (a c)"), pA[1][:].rearrange("p a c -> p (a c)"),
                    pJ[0][:], pJ[1][:]]
            ybank = [pO[0][:, 0, :], pO[1][:, 0, :]]
            rows_transposed(0)
            ends = [pe.value_load(cum_i[0:1, e:e + 1], min_val=e + 1, max_val=TILES) for e in range(E)]
            for e in range(E):
                with pe.Fori(0 if e == 0 else ends[e - 1], ends[e]) as t:
                    pe.wait_ge(xt_ready, t + 1)
                    for f in range(FB):
                        pe.wait_ge(h_ready, FIRST + t * FB)
                        mm(bank[f][:, 0:ROWS], wgate_sb[:, e, f * P:(f + 1) * P], xtT[:], start=True, stop=True)
                        mm(bank[f][:, ROWS:2 * ROWS], wup_sb[:, e, f * P:(f + 1) * P], xtT[:],
                           start=True, stop=True).then_inc(up_psum, 1)
                    rows_transposed(t + 1)
                    pe.wait_ge(y_ready, FIRST + t * 2)
                    for f in range(FB):
                        pe.wait_ge(h_ready, FIRST + t * FB + f + 1)
                        for k in range(2):
                            last = mm(ybank[k], hT[:, f, k * P:(k + 1) * P], wdown_sb[:, e, f, :],
                                      start=(f == 0), stop=(f == FB - 1))
                    last.then_inc(y_psum, 1)

        @block.scalar
        def _(act):
            a = nc.scalar.activation

            def eps(col):
                return cst[:, col:col + 1]

            def norm_rstd(j):
                act.wait_ge(xn_stat, j * 2 * NT + 2 * NT)
                a(lnv[:, 0, :], mv[:, 0, :, 1], ACT.Ln, bias=eps(C_EPS_LN)).then_inc(xn_lnv, 1)
                act.wait_ge(xn_lnv, j + 1)
                a(rstd[:, 0, :], lnv[:, 0, :], ACT.Exp, scale=-0.5).then_inc(xn_rstd, 1)

            def norm_T(j):
                act.wait_ge(xnT_psum, j + 1)
                for k in range(2):
                    a(xnT[:, :, k, :], pW[:].rearrange("p (n c) -> p n c", c=C), ACT.Copy)\
                        .then_inc(xnT_ready, 1)

            def gates(j):
                if not at_start(j):
                    act.wait_ge(run_ready, j)
                for p in range(PAIRS):
                    act.wait_ge(z_psum, j * 2 + p + 1)
                    a(absz[:, p, :], pJ[p][:], ACT.Abs, bias=bg2_sb[:, p:p + 1]).then_inc(absz_ready, 1)
                    a(relz[:, p, :], pJ[p][:], ACT.Relu, scale=-1.0, bias=nbg2_sb[:, p:p + 1])\
                        .then_inc(relz_ready, 1)

            def gate_logs(j):
                act.wait_ge(absz_ready, j * 2 + 2)
                a(absz[:], absz[:], ACT.Exp, scale=-1.0).then_inc(ez_ready, 1)
                act.wait_ge(ez_ready, j + 1)
                a(absz[:], absz[:], ACT.Ln, bias=1.0).then_inc(lz_ready, 1)

            def decays(j):
                act.wait_ge(rel_ready, j + 1)
                a(shrink[:], rel[:], ACT.Exp, scale=1.0 / GATE_NORMALIZER).then_inc(decay_ready, 1)
                a(grow[:], rel[:], ACT.Exp, scale=-1.0 / GATE_NORMALIZER).then_inc(decay_ready, 1)
                act.wait_ge(steplog_ready, j + 1)
                a(step[:, :, 0:NC - 1], step_log[:, :, 0:NC - 1], ACT.Exp,
                  scale=-1.0 / GATE_NORMALIZER).then_inc(step_ready, 1)

            def values(j):
                for g in range(NC // 2):
                    act.wait_ge(v_psum, j * 4 + g + 1)
                    for half in range(2):
                        rows = slice(half * D, half * D + D)
                        a(vJ[rows, 2 * g:2 * g + 2, :, half * D:half * D + D].rearrange("p c q d -> p (c q) d"),
                          four[g][rows, :].rearrange("p (n h d) -> p n h d", h=2, d=D)[:, :, half, :],
                          ACT.Copy).then_inc(v_ready, 1)

            def keys(j):
                for g in range(NC // 2):
                    act.wait_ge(kJ_psum, j * 4 + g + 1)
                    n = min(2, NC - 1 - 2 * g)
                    a(kJ[:, 2 * g:2 * g + n, :, :].rearrange("p c q j -> p (c q j)"), key_bank[g][:, 0:n * 2 * P],
                      ACT.Copy).then_inc(kJ_ready, 1)

            def head_norm(i, c):
                act.wait_ge(o_psum, i * NC + c + 1)
                a(sq[:, c % 2, :], pO[c % 2][:].rearrange("p k v -> p (k v)"), ACT.Square)\
                    .then_inc(sq_ready, 1)
                if c > 0:
                    out_T(i, c - 1)
                act.wait_ge(ss_ready, i * NC + c + 1)
                a(lnss[:, c % 2, :], ss[:, c % 2, :], ACT.Ln, scale=1.0 / D, bias=eps(C_EPS_HEAD))\
                    .then_inc(lnss_ready, 1)
                act.wait_ge(lnss_ready, i * NC + c + 1)
                a(rs[:, c % 2, :], lnss[:, c % 2, :], ACT.Exp, scale=-0.5).then_inc(rs_ready, 1)

            def out_T(i, c):
                act.wait_ge(ot_psum, i * NC + c + 1)
                a(oT[:, (c // 2) % 2, :, c % 2, :], pT[:].rearrange("p (b c) -> p b c", c=C), ACT.Copy,
                  scale=gn_sb[:, 0:1]).then_inc(ot_ready, 1)

            def merged_rstd(i, t):
                act.wait_ge(w_stat, (i * NT + t) * 2 + 2)
                a(lnv[:, 1, t:t + 1], mv[:, 1, t, 1:2], ACT.Ln, bias=eps(C_EPS_LN)).then_inc(w_lnv, 1)
                act.wait_ge(w_lnv, i * NT + t + 1)
                a(rstd[:, 1, t:t + 1], lnv[:, 1, t:t + 1], ACT.Exp, scale=-0.5).then_inc(w_rstd, 1)

            def chunks(i, more, routed):
                for c in range(NC):
                    if routed and c == 2:
                        router_T(i - 1)
                    if more and c == 5:
                        gates(i + 1)
                    head_norm(i, c)
                    if routed and c == 0:
                        router_rstd(i - 1)
                    if more and c == 1:
                        norm_rstd(i + 1)
                    if more and c == 2:
                        norm_T(i + 1)
                    if routed and c == 3:
                        act.wait_ge(diff_ready, i)
                        a(ediff[:], diff[:], ACT.Exp).then_inc(ediff_ready, 1)
                    if more and c == 5:
                        gate_logs(i + 1)
                    if more and c == 7:
                        decays(i + 1)
                    if c in (3, 5, 7):
                        merged_rstd(i, (c - 3) // 2)

            def router_rstd(i):
                act.wait_ge(r_aggr, i * NT + NT)
                a(lnv[:, 2, :], mv[:, 2, :, 1], ACT.Ln, bias=eps(C_EPS_LN)).then_inc(r_lnv, 1)
                act.wait_ge(r_lnv, i + 1)
                a(rstd[:, 2, :], lnv[:, 2, :], ACT.Exp, scale=-0.5).then_inc(r_rstd, 1)

            def router_T(i):
                act.wait_ge(x1nT_psum, i + 1)
                a(x1nT[:].rearrange("p t j -> p (t j)"), pW[:], ACT.Copy).then_inc(x1nT_ready, 1)

            act.wait_ge(weights_in, 16 * len(WEIGHTS))
            act.wait_ge(vJ_zero, 1)
            act.wait_ge(const_made, 8)
            act.preload_act_table_set(LOG_EXP)
            norm_rstd(0)
            norm_T(0)
            gates(0)
            gate_logs(0)
            decays(0)
            values(0)
            keys(0)

            def turn(i, routed):
                chunks(i, True, routed)
                out_T(i, NC - 1)
                values(i + 1)
                keys(i + 1)
                merged_rstd(i, NT - 1)

            turn(0, False)
            with act.Fori(1, S - 1) as i:
                act.preload_act_table_set(LOG_EXP)
                turn(i, True)
            act.preload_act_table_set(LOG_EXP)
            chunks(S - 1, False, True)
            out_T(S - 1, NC - 1)
            merged_rstd(S - 1, NT - 1)
            router_rstd(S - 1)
            router_T(S - 1)
            act.wait_ge(diff_ready, S)
            a(ediff[:], diff[:], ACT.Exp).then_inc(ediff_ready, 1)

            act.wait_ge(counts_ready, 1)
            total = act.value_load(cum_i[0:1, E - 1:E], min_val=E, max_val=TILES)
            bank = [pA[0][:].rearrange("p a c -> p (a c)"), pA[1][:].rearrange("p a c -> p (a c)"),
                    pJ[0][:], pJ[1][:]]
            act.wait_ge(xt_psum, 1)
            a(xtT[:], pT[:, 0:ROWS], ACT.Copy).then_inc(xt_ready, 1)
            with act.Fori(0, total) as t:
                for f in range(FB):
                    act.wait_ge(up_psum, t * FB + f + 1)
                    act.wait_ge(h_ready, FIRST + t * FB)
                    a(sil[:, f, :], bank[f][:, 0:ROWS], ACT.Silu).then_inc(silu_ready, 1)
                act.wait_ge(xt_psum, t + 2)
                a(xtT[:], pT[:, 0:ROWS], ACT.Copy).then_inc(xt_ready, 1)
                act.wait_ge(y_psum, FIRST + t + 1)
                act.wait_ge(y_free, FIRST + t)
                act.wait_ge(tail_kept, FIRST + t + 1)
                for k in range(2):
                    a(y[:, k, :], pO[k][:, 0, :], ACT.Copy, scale=tail[:, k, 0:1]).then_inc(y_ready, 1)

            act.preload_act_table_set(LOG_EXP)
            with act.Fori(0, S // 2) as n:
                for b in range(2):
                    i = n * 2 + b
                    act.wait_ge(c_stat, i * 2 * NT + 2 * NT)
                    a(lnv[:, b, :], mv[:, b, :, 1], ACT.Ln, bias=eps(C_EPS_LN)).then_inc(c_lnv, 1)
                    act.wait_ge(c_lnv, i + 1)
                    a(rstd[:, b, :], lnv[:, b, :], ACT.Exp, scale=-0.5).then_inc(c_rstd, 1)
                    act.wait_ge(c_res, i + 1)
                    act.dma_start(seq(ov, i), cbuf[:, b, 3, :, :]).then_inc(c_out, 16)

        @block.vector
        def _(dve):
            v = nc.vector

            def norm_stats(j):
                dve.wait_ge(xa_in, j * 16 + 16)
                for t in range(NT):
                    v.bn_stats(st[:, 0, t, :], xa[:, t, :]).then_inc(xn_stat, 1)
                dve.wait_ge(xn_stat, j * 2 * NT + NT)
                settle(dve)
                for t in range(NT):
                    v.bn_aggr(mv[:, 0, t, :], st[:, 0, t, :]).then_inc(xn_stat, 1)

            def norm_apply(j):
                dve.wait_ge(xn_rstd, j + 1)
                for t in range(NT):
                    v.tensor_scalar(xn[:, t, :], xa[:, t, :], mv[:, 0, t, 0:1], rstd[:, 0, t:t + 1],
                                    ALU.subtract, ALU.mult).then_inc(xn_ready, 1)

            def gate_copy(j):
                dve.wait_ge(h1_psum, j + 1)
                v.tensor_copy(h1[:], pJ[0][0:LOW, :]).then_inc(h1_ready, 1)

            def gate_sums(j):
                dve.wait_ge(lz_ready, j + 1)
                dve.wait_ge(relz_ready, j * 2 + 2)
                v.tensor_tensor(relz[:], relz[:], absz[:], ALU.add).then_inc(gate_ready, 1)
                dve.wait_ge(gate_ready, j + 1)
                v.tensor_tensor_scan(run[:].rearrange("p a l -> p (a l)"), in_chunk,
                                     relz[:].rearrange("p a l -> p (a l)"), 0.0, ALU.mult, ALU.add)\
                    .then_inc(run_ready, 1)

            def gate_relative(j):
                dve.wait_ge(run_ready, j + 1)
                mid = C // 2 - 1
                r4 = run[:].rearrange("p a (n c) -> p (a n) c", c=C)
                v.tensor_tensor(rel[:].rearrange("p a (n c) -> p (a n) c", c=C), r4,
                                wide(r4[:, :, mid:mid + 1], P, PAIRS * NC, C), ALU.subtract)\
                    .then_inc(rel_ready, 1)
                dve.wait_ge(rel_ready, j + 1)
                rn = run[:].rearrange("p a (n c) -> p a n c", c=C)
                ln = rel[:].rearrange("p a (n c) -> p a n c", c=C)
                v.tensor_tensor(step_log[:, :, 0:NC - 1], ln[:, :, 0:NC - 1, C - 1], rn[:, :, 1:NC, mid], ALU.add)\
                    .then_inc(steplog_ready, 1)

            def keys(j):
                dve.wait_ge(decay_ready, j * 2 + 2)
                for p in range(PAIRS):
                    dve.wait_ge(k_psum, j * 2 + p + 1)
                    for half in range(2):
                        rows = slice(half * D, half * D + D)
                        v.scalar_tensor_tensor(
                            out=kT[rows, p, :, half * C:half * C + C],
                            in0=pJ[p][rows, :].rearrange("p (n c) -> p n c", c=C), scalar=0.0,
                            in1=shrink[rows, p, :].rearrange("p (n c) -> p n c", c=C),
                            op0=ALU.max, op1=ALU.mult).then_inc(k_ready, 1)

            def query(j, b):
                dve.wait_ge(q_psum, j * 8 + b + 1)
                v.scalar_tensor_tensor(
                    out=qT[:, b // R, :, b % R, :], in0=four[b % 4].rearrange("p (n c) -> p n c", c=C),
                    scalar=0.0, in1=grow[:, b // R, :].rearrange("p (n c) -> p n c", c=C),
                    op0=ALU.max, op1=ALU.mult).then_inc(q_ready, 1)

            def state(j, c):
                dve.wait_ge(step_ready, j + 1)
                dve.wait_ge(upd_psum, j * (NC - 1) + c + 1)
                if c >= 2:
                    dve.wait_ge(mid_ready, j * (NC - 1) + c - 1)
                if c == 0:
                    v.tensor_copy(S_raw[:, 0, :, :], pO[0][:, 0:PAIRS, :]).then_inc(raw_ready, 1)
                else:
                    dve.wait_ge(raw_ready, j * (NC - 1) + c)
                    for p in range(PAIRS):
                        ins = v.scalar_tensor_tensor(
                            out=S_raw[:, c % 2, p, :], in0=S_raw[:, (c - 1) % 2, p, :],
                            scalar=step[:, p, c - 1:c], in1=pO[c % 2][:, p, :], op0=ALU.mult, op1=ALU.add)
                    ins.then_inc(raw_ready, 1)

            def queries_and_states(j, merging):
                for n in range(2 * PAIRS * R):
                    if query_turn(n) is not None:
                        query(j, query_turn(n))
                    if state_turn(n) is not None:
                        state(j, state_turn(n))
                    if n == 1 and merging is not None:
                        merged(merging, NT - 1)

            def mask(i, c):
                dve.wait_ge(a_psum, i * NC + c + 1)
                v.tensor_tensor(
                    aT[:, c % 2, :, :].rearrange("p a (r c) -> p (a r) c", c=C),
                    pA[c % 2][:].rearrange("p a (r c) -> p (a r) c", c=C),
                    wide(causal.unsqueeze(1), P, PAIRS * R, C), ALU.mult).then_inc(a_ready, 1)

            def head_norm(i, c):
                dve.wait_ge(sq_ready, i * NC + c + 1)
                v.tensor_reduce(ss[:, c % 2, :], sq[:, c % 2, :].rearrange("p (n d) -> p n d", d=D), AX, ALU.add)\
                    .then_inc(ss_ready, 1)
                if c + 1 < NC:
                    mask(i, c + 1)
                dve.wait_ge(rs_ready, i * NC + c + 1)
                v.tensor_tensor(
                    on[:, c % 2, :, :].rearrange("p k (h d) -> p (k h) d", d=D),
                    pO[c % 2][:].rearrange("p k (h d) -> p (k h) d", d=D),
                    wide(rs[:, c % 2, :].unsqueeze(2), P, 8, D), ALU.mult).then_inc(on_ready, 1)

            def merged(i, t):
                n = i * NT + t
                dve.wait_ge(w_psum, n + 1)
                v.bn_stats(st[:, 1, t, :], pW[:, 0:HID]).then_inc(w_stat, 1)
                dve.wait_ge(w_stat, n * 2 + 1)
                settle(dve)
                v.bn_aggr(mv[:, 1, t, :], st[:, 1, t, :]).then_inc(w_stat, 1)
                dve.wait_ge(w_rstd, n + 1)
                dve.wait_ge(x1_ready, FIRST + i * NT)
                v.tensor_scalar(an[:, t, :], pW[:, 0:HID], mv[:, 1, t, 0:1], rstd[:, 1, t:t + 1],
                                ALU.subtract, ALU.mult).then_inc(an_ready, 1)

            def chunks(i, more, routed):
                mask(i, 0)
                for c in range(NC):
                    if routed and c == 0:
                        router_stats(i - 1)
                    if routed and c == 1:
                        router_norm(i - 1)
                    if more and c == 1:
                        norm_stats(i + 1)
                    if more and c == 2:
                        norm_apply(i + 1)
                    if routed and c == 3:
                        choose(i - 1)
                    if more and c == 4:
                        gate_copy(i + 1)
                    if routed and c == 4:
                        places(i - 1)
                    if routed and c == 5:
                        weigh(i - 1)
                    if more and c == 6:
                        gate_sums(i + 1)
                    if more and c == 7:
                        dve.wait_ge(mid_ready, i * (NC - 1) + NC - 1)
                        gate_relative(i + 1)
                    head_norm(i, c)
                    if c in (3, 5, 7):
                        merged(i, (c - 3) // 2)

            def router_stats(i):
                dve.wait_ge(x1_ready, FIRST + i * NT + NT)
                for t in range(NT):
                    v.bn_stats(st[:, 2, t, :], x1[:, t, :]).then_inc(r_stat, 1)
                dve.wait_ge(r_stat, i * NT + NT)
                settle(dve)
                for t in range(NT):
                    v.bn_aggr(mv[:, 2, t, :], st[:, 2, t, :]).then_inc(r_aggr, 1)

            def router_norm(i):
                dve.wait_ge(r_rstd, i + 1)
                dve.wait_ge(rows_free, FIRST + i)
                for t in range(NT):
                    v.tensor_scalar(x1n[:, 0, t, 0:HID], x1[:, t, :], mv[:, 2, t, 0:1], rstd[:, 2, t:t + 1],
                                    ALU.subtract, ALU.mult).then_inc(x1n_ready, 1)

            def choose(i):
                dve.wait_ge(logit_psum, i + 1)
                v.tensor_tensor(logit[:], pJ[1][:, 0:NT * E].rearrange("p (t e) -> p t e", e=E),
                                wide(rb_sb[:].unsqueeze(1), P, NT, E), ALU.add).then_inc(logit_ready, 1)
                dve.wait_ge(logit_ready, i + 1)
                settle(dve)
                for t in range(NT):
                    v.max(top[:, t, :], logit[:, t, :]).then_inc(top_ready, 1)
                dve.wait_ge(top_ready, i * NT + NT)
                settle(dve)
                for t in range(NT):
                    v.max_index(top_i[:, t, :], top[:, t, :], logit[:, t, :]).then_inc(topi_ready, 1)
                v.tensor_tensor(diff[:], top[:, :, 1], top[:, :, 0], ALU.subtract).then_inc(diff_ready, 1)
                dve.wait_ge(topi_ready, i * NT + NT)
                v.tensor_copy(top_f[:], top_i[:]).then_inc(topf_ready, 1)
                dve.wait_ge(topf_ready, i + 1)
                for k in range(2):
                    v.tensor_tensor(pick[:, k, :, :], wide(iota8.unsqueeze(1), P, NT, E),
                                    wide(top_f[:, :, k:k + 1], P, NT, E), ALU.is_equal).then_inc(pick_ready, 1)
                dve.wait_ge(pick_ready, i * 2 + 2)
                v.tensor_tensor(both[:], pick[:, 0, :, :], pick[:, 1, :, :], ALU.add).then_inc(both_ready, 1)

            def weigh(i):
                dve.wait_ge(ediff_ready, i + 1)
                v.tensor_scalar(den[:], ediff[:], 1.0, None, ALU.add).then_inc(den_ready, 1)
                dve.wait_ge(den_ready, i + 1)
                v.reciprocal(gts[:, 0, :], den[:]).then_inc(g1_ready, 1)
                dve.wait_ge(g1_ready, i + 1)
                v.tensor_tensor(gts[:, 1, :], gts[:, 0, :], ediff[:], ALU.mult).then_inc(g2_ready, 1)
                dve.wait_ge(g2_ready, i + 1)
                v.tensor_copy(x1n[:, :, :, HID], gts[:]).then_inc(tail_ready, 1)
                v.tensor_copy(x1n[:].bitcast(U32)[:, :, :, HID + 1], goal[:]).then_inc(tail_ready, 1)
                dve.wait_ge(tail_ready, i * 2 + 2)
                v.tensor_scalar(goal[:], goal[:], float(L), None, ALU.add).then_inc(goal_ready, 1)

            def places(i):
                dve.wait_ge(rank_psum, i + 1)
                dve.wait_ge(base_ready, FIRST + i)
                v.tensor_tensor(place[:], pJ[1][:, 0:NT * E].rearrange("p (t e) -> p t e", e=E),
                                wide(base[:].unsqueeze(1), P, NT, E), ALU.add).then_inc(place_ready, 1)
                dve.wait_ge(place_ready, i + 1)
                v.tensor_tensor(base[:], base[:], pJ[1][:, NT * E:(NT + 1) * E], ALU.add).then_inc(base_ready, 1)
                v.tensor_tensor(placed[:], pick[:], wide(place[:].unsqueeze(1), P, 2, NT, E), ALU.mult)\
                    .then_inc(placed_ready, 1)
                dve.wait_ge(placed_ready, i + 1)
                v.tensor_reduce(rowf[:], placed[:], AX, ALU.add).then_inc(rowf_ready, 1)
                dve.wait_ge(rowf_ready, i + 1)
                v.tensor_copy(rowi[:], rowf[:]).then_inc(rowi_ready, 1)

            dve.wait_ge(weights_in, 16 * len(WEIGHTS))
            v.tensor_copy(tri[:], cst[:, C_TRI:C_TRI + P]).then_inc(const_made, 1)
            v.memset(ones[:], 1.0).then_inc(const_made, 1)
            v.tensor_copy(base[:], cst[:, C_BASE:C_BASE + E]).then_inc(const_made, 1)
            v.tensor_copy(goal[:].rearrange("p k t -> p (k t)"), cst[:, C_GOAL:C_GOAL + 8]).then_inc(const_made, 1)
            v.memset(zeros[:], 0.0).then_inc(const_made, 1)
            v.memset(kT[:], 0.0).then_inc(const_made, 1)
            v.tensor_scalar(nbg2_sb[:], bg2_sb[:], -1.0, None, ALU.mult).then_inc(const_made, 1)
            dve.wait_ge(const_made, 7)
            v.tensor_copy(zeros[:].bitcast(U32)[:, :, HID + 1], cst[:, C_PAD:C_PAD + 2]).then_inc(const_made, 1)
            norm_stats(0)
            norm_apply(0)
            gate_copy(0)
            gate_sums(0)
            gate_relative(0)
            keys(0)
            queries_and_states(0, None)

            def turn(i, routed):
                chunks(i, True, routed)
                keys(i + 1)
                queries_and_states(i + 1, i)

            turn(0, False)
            with dve.Fori(1, S - 1) as i:
                turn(i, True)
            chunks(S - 1, False, True)
            merged(S - 1, NT - 1)
            router_stats(S - 1)
            router_norm(S - 1)
            choose(S - 1)
            weigh(S - 1)
            places(S - 1)

            steps = [0]

            def link(ins):
                steps[0] += 1
                ins.then_inc(dve_step, 1)
                dve.wait_ge(dve_step, steps[0])

            dve.wait_ge(base_ready, FIRST + S)
            link(v.tensor_copy(end_i[:], base[:]))
            link(v.tensor_tensor(cnt[:], base[:], cst[:, C_BASE:C_BASE + E], ALU.subtract))
            link(v.tensor_scalar(cnt[:], cnt[:], float(ROWS - 1), None, ALU.add))
            link(v.tensor_copy(cnt_i[:], cnt[:]))
            link(v.tensor_scalar(til_i[:], cnt_i[:], ROWS.bit_length() - 1, None, ALU.arith_shift_right))
            link(v.tensor_copy(til[:], til_i[:]))
            link(v.tensor_scalar(til[:], til[:], 1.0, None, ALU.max))
            link(v.tensor_tensor_scan(cum[:], ones_row, til[:], 0.0, ALU.mult, ALU.add))
            link(v.tensor_copy(cum_i[:], cum[:]))
            n1 = TILES + 1
            link(v.tensor_tensor(tge[:], wide(tnum.unsqueeze(2), 1, n1, E),
                                 wide(cum[0:1, :].unsqueeze(1), 1, n1, E), ALU.is_ge))
            link(v.tensor_tensor(tmul[:], tge[:], wide(til[0:1, :].unsqueeze(1), 1, n1, E), ALU.mult))
            link(v.tensor_reduce(te[:], tge[:], AX, ALU.add))
            link(v.tensor_reduce(tprev[:], tmul[:], AX, ALU.add))
            link(v.tensor_tensor(trow[:], tnum, tprev[:], ALU.subtract))
            link(v.tensor_scalar(trow[:], trow[:], float(ROWS), None, ALU.mult))
            link(v.scalar_tensor_tensor(out=trow[:], in0=te[:], scalar=float(CAP), in1=trow[:],
                                        op0=ALU.mult, op1=ALU.add))
            link(v.tensor_scalar(trow[:], trow[:], float(E * CAP), None, ALU.min))
            v.tensor_copy(trow_i[:], trow[:]).then_inc(counts_ready, 1)
            dve.wait_ge(counts_ready, 1)

            dve.wait_ge(xt_in, 16)
            v.tensor_copy(tail_next[:].bitcast(U32), xt[:, :, HID:XW].bitcast(U32)).then_inc(tail_next_ready, 1)
            total = dve.value_load(cum_i[0:1, E - 1:E], min_val=E, max_val=TILES)
            bank = [pA[0][:].rearrange("p a c -> p (a c)"), pA[1][:].rearrange("p a c -> p (a c)"),
                    pJ[0][:], pJ[1][:]]
            with dve.Fori(0, total) as t:
                for f in range(FB):
                    dve.wait_ge(silu_ready, t * FB + f + 1)
                    if f == 0:
                        dve.wait_ge(y_psum, FIRST + t)
                    v.tensor_tensor(hT[:, f, :], bank[f][:, ROWS:2 * ROWS], sil[:, f, :], ALU.mult)\
                        .then_inc(h_ready, 1)
                dve.wait_ge(y_free, FIRST + t)
                dve.wait_ge(tail_next_ready, t + 1)
                v.tensor_copy(tail[:].bitcast(U32), tail_next[:].bitcast(U32)).then_inc(tail_kept, 1)
                dve.wait_ge(tail_kept, FIRST + t + 1)
                dve.wait_ge(xt_in, t * 16 + 32)
                v.tensor_copy(tail_next[:].bitcast(U32), xt[:, :, HID:XW].bitcast(U32)).then_inc(tail_next_ready, 1)

            with dve.Fori(0, S // 2) as n:
                for b in range(2):
                    i = n * 2 + b
                    dve.wait_ge(c_in[b], n * 48 + 48)
                    v.tensor_tensor(cn[:, b, :, :], cbuf[:, b, 0, :, :], cbuf[:, b, 1, :, :], ALU.add)\
                        .then_inc(c_sum, 1)
                    dve.wait_ge(c_sum, i + 1)
                    for t in range(NT):
                        v.bn_stats(st[:, b, t, :], cn[:, b, t, :]).then_inc(c_stat, 1)
                    dve.wait_ge(c_stat, i * 2 * NT + NT)
                    settle(dve)
                    for t in range(NT):
                        v.bn_aggr(mv[:, b, t, :], st[:, b, t, :]).then_inc(c_stat, 1)
                    dve.wait_ge(c_rstd, i + 1)
                    for t in range(NT):
                        v.tensor_scalar(cn[:, b, t, :], cn[:, b, t, :], mv[:, b, t, 0:1], rstd[:, b, t:t + 1],
                                        ALU.subtract, ALU.mult).then_inc(c_norm, 1)
                    dve.wait_ge(c_norm, i * NT + NT)
                    dve.wait_ge(c_out_before, FIRST + i)
                    v.tensor_tensor(cbuf[:, b, 3, :, :], cn[:, b, :, :], cbuf[:, b, 2, :, :], ALU.add).then_inc(c_res, 1)

        @block.gpsimd
        def _(pool):
            g = nc.gpsimd

            def mids(j, merging=None):
                pool.wait_ge(step_ready, j + 1)
                settle(pool)
                for c in range(NC - 1):
                    pool.wait_ge(raw_ready, j * (NC - 1) + c + 1)
                    settle(pool)
                    g.tensor_tensor(S_mid[:, c + 1, :, :], S_raw[:, c % 2, :, :],
                                    wide(step[:, :, c:c + 1], P, PAIRS, P), ALU.mult).then_inc(mid_ready, 1)
                    if c == 1 and merging is not None:
                        residual(merging, NT - 1)

            def residual(i, t):
                pool.wait_ge(an_ready, i * NT + t + 1)
                settle(pool)
                pool.wait_ge(xr_in, i * 16 + 16)
                settle(pool)
                if t == 0:
                    pool.wait_ge(x1_out, FIRST + i * 16)
                    settle(pool)
                    pool.wait_ge(x1n_ready, FIRST + i * NT)
                    settle(pool)
                g.tensor_tensor(x1[:, t, :], an[:, t, :], xr[:, t, :], ALU.add).then_inc(x1_ready, 1)

            def copy_rows(i):
                pool.wait_ge(x1n_ready, FIRST + i * NT + NT)
                settle(pool)
                g.tensor_copy(x1n[:, 1, :, 0:HID], x1n[:, 0, :, 0:HID]).then_inc(copied, 1)
                pool.wait_ge(copied, i + 1)
                settle(pool)

            def scatter(i):
                pool.wait_ge(tail_ready, i * 2 + 2)
                settle(pool)
                pool.wait_ge(rowi_ready, i + 1)
                settle(pool)
                for t in range(NT):
                    for k in range(2):
                        g.indirect_dma_start(out=xs_dram, in_=x1n[:, k, t, :], in_offset=None,
                                             out_offset=bass.IndirectOffsetOnAxis(ap=rowi[:, k, t:t + 1], axis=0))\
                            .then_inc(scattered, 16)

            def scattered_all(i):
                pool.wait_ge(scattered, (i + 1) * (16 * 2 * NT))
                pool.sem_inc(rows_free, 1)

            g.memset(vJ[:], 0.0).then_inc(vJ_zero, 1)
            mids(0)

            def turn(i, routed):
                if routed:
                    copy_rows(i - 1)
                residual(i, 0)
                if routed:
                    scatter(i - 1)
                for t in range(1, NT - 1):
                    residual(i, t)
                if routed:
                    scattered_all(i - 1)

            turn(0, False)
            mids(1, 0)
            with pool.Fori(1, S - 1) as i:
                turn(i, True)
                mids(i + 1, i)
            turn(S - 1, True)
            residual(S - 1, NT - 1)
            copy_rows(S - 1)
            scatter(S - 1)

            pool.wait_ge(counts_ready, 1)
            total = pool.value_load(cum_i[0:1, E - 1:E], min_val=E, max_val=TILES)
            with pool.Fori(0, total) as t:
                pool.wait_ge(y_ready, FIRST + t * 2 + 2)
                settle(pool)
                for k in range(2):
                    g.indirect_dma_start(
                        out=ys_dram, in_=y[:, k, :], in_offset=None,
                        out_offset=bass.IndirectOffsetOnAxis(ap=tail[:, k, 1:2].bitcast(U32), axis=0))\
                        .then_inc(y_out, 16)
                pool.wait_ge(y_out, t * 32 + 32)
                pool.sem_inc(y_free, 1)

            with pool.Fori(0, S // 2) as n:
                for b in range(2):
                    pool.wait_ge(c_out, n * 32 + b * 16 + 16)
                    pool.sem_inc(c_out_before, 1)



def kernel(**inputs):
    import concourse.bacc as _bacc
    from concourse.bass_utils import run_bass_kernel_spmd as _run

    g = {n.removeprefix("L0_"): np.asarray(a) for n, a in inputs.items()}
    x = np.ascontiguousarray(g["attn_hidden_states"])
    tiles = 2 * x.shape[0] * x.shape[1] // ROWS + E
    cap = x.shape[0] * x.shape[1] + ROWS
    c = np.zeros((P, C_TNUM + tiles + 1), np.float32)
    c[:, C_IDENT:C_IDENT + P] = np.eye(P)
    c[:, C_MASK:C_MASK + C] = np.tile(np.triu(np.ones((C, C))), (2, 1))
    c[:, C_TRI:C_TRI + P] = np.triu(np.ones((P, P)), 1)
    c[:, C_IOTA:C_IOTA + E] = np.arange(E)
    c[:, C_SCAN:C_SCAN + 1024] = np.arange(1024) % C != 0
    c[:, C_EPS_HEAD] = D * NORM_EPS
    c[:, C_EPS_LN] = LN_EPS
    c[:, C_BASE:C_BASE + E] = np.arange(E) * cap
    c[:, C_ONES:C_ONES + E] = 1
    tokens = x.shape[0] * x.shape[1]
    c[:, C_GOAL:C_GOAL + 8] = np.arange(P)[:, None] + (np.arange(2)[:, None] * tokens + np.arange(4) * P).reshape(8)
    c[:, C_PAD:C_PAD + 2] = 2 * tokens + np.arange(P)[:, None] + np.arange(2) * P
    c[:, C_TNUM:] = np.arange(tiles + 1)
    arrays = {
        "x": x,
        "wq": g["attn_Wq"].reshape(HID, PAIRS, 2, R, D).transpose(0, 1, 3, 2, 4).reshape(HID, PAIRS, R, P),
        "wk": g["attn_Wk"].reshape(HID, PAIRS, P),
        "wv": g["attn_Wv"],
        "wo": g["attn_Wo"].reshape(PAIRS, 2, R, D, HID).transpose(1, 3, 0, 2, 4).reshape(P, PAIRS * R, HID),
        "wg1": g["attn_Wg1"],
        "wg2": g["attn_Wg2"].reshape(LOW, PAIRS, P),
        "bg2": g["attn_bg2"].reshape(PAIRS, P).T,
        "gnorm": np.concatenate([g["attn_g_norm_weight"]] * 2).reshape(P, 1),
        "rw": g["ffn_router_w"].T,
        "rb": g["ffn_router_b"].reshape(1, E),
        "wgate": g["ffn_gate_w"].transpose(2, 0, 1),
        "wup": g["ffn_up_w"].transpose(2, 0, 1),
        "wdown": g["ffn_down_w"].reshape(E, HID, FB, P).transpose(3, 0, 2, 1),
        "consts": c,
    }
    arrays = {n: np.ascontiguousarray(a) for n, a in arrays.items()}
    nc = _bacc.Bacc("TRN2", target_bir_lowering=False, num_devices=1)
    args = [nc.dram_tensor(n, a.shape, F32, kind="ExternalInput").ap() for n, a in arrays.items()]
    out = nc.dram_tensor("out", x.shape, F32, kind="ExternalOutput").ap()
    build(nc, *args, out)
    r = _run(nc, [arrays], core_ids=[0])
    return r.results[0]["out"]
```
